# Optimizing a Trainium2 kernel written in Bass

```python
import numpy as np
import jax
import jax.numpy as jnp

def _softmax(x, axis=-1):
    return jax.nn.softmax(x, axis=axis)

def _gelu(x):
    return jax.nn.gelu(x, approximate=True)

def _silu(x):
    return jax.nn.silu(x)

def _sigmoid(x):
    return jax.nn.sigmoid(x)

def _layernorm(x, axis=-1, eps=1e-05):
    m = jnp.mean(x, axis=axis, keepdims=True)
    v = jnp.var(x, axis=axis, keepdims=True)
    return (x - m) / jnp.sqrt(v + eps)

def _scatter_add(tgt, idx, src, axis=0):
    return tgt.at[idx].add(src)

def _segment_sum(src, seg, n):
    return jax.ops.segment_sum(src, seg, n)
kernel_name = 'mk_gnn_resnorm_d1_gnn_r8_62e729'

def setup_inputs(seed: int=0):
    np.random.seed(seed)
    _w = jnp.asarray

    def _rec_inputs():
        import jax
        import jax.numpy as jnp
        _gk = jax.random.key(seed)
        x = 7.22e-05 + 1 * jax.random.normal(jax.random.fold_in(_gk, 1), (6250, 256), jnp.float32)
        src = jax.random.randint(jax.random.fold_in(_gk, 2), (200000,), 0, 6250, jnp.int32)
        dst = jnp.minimum((6250 * jax.random.uniform(jax.random.fold_in(_gk, 3), (200000,)) ** 2.0).astype(jnp.int32), 49999)
        _o = jnp.argsort(dst, stable=True)
        src = src[_o]
        dst = dst[_o]
        edge_attr_5 = jax.random.uniform(jax.random.fold_in(_gk, 11), (200000, 5), jnp.float32, 0.0, 99.9996)
        node_type_19 = jax.random.randint(jax.random.fold_in(_gk, 13), (6250,), 0, 19, jnp.int32)
        return (x, src, dst, edge_attr_5, node_type_19)
    x, src, dst, edge_attr_5, node_type_19 = _rec_inputs()

    def _L0_gnn_setup():
        import jax, jax.numpy as jnp
        import numpy as np
        N = 4096
        E = 16384
        IN = 256
        OUT = 256
        TD = 32
        H = 4
        T = 19
        PROJ = OUT - 2 * TD
        DK = (OUT - TD) // H
        SQRT_DK = float(np.sqrt(DK))
        LN_EPS = 1e-05

        def time_emb(t, w, b):
            return jnp.cos(jnp.log(t + 1.0)[:, None] * w[None, :] + b[None, :])

        def typed_linear(x, W, b, node_type):
            out = jnp.zeros((x.shape[0], W.shape[2]), x.dtype)
            for t in range(W.shape[0]):
                out = jnp.where((node_type == t)[:, None], x @ W[t] + b[t], out)
            return out

        def seg_softmax(att, idx, n):
            m = jax.ops.segment_max(att, idx, num_segments=n)
            e = jnp.exp(att - m[idx])
            s = jax.ops.segment_sum(e, idx, num_segments=n)
            return e / (s[idx] + 1e-16)
        key = jax.random.key(seed)
        ks = jax.random.split(key, 8)
        x = jax.random.normal(ks[0], (N, IN), jnp.float32)
        node_type = jax.random.randint(ks[1], (N,), 0, T, jnp.int32)
        edge_index = jax.random.randint(ks[2], (2, E), 0, N, jnp.int32)
        times = jax.random.uniform(ks[3], (E, 3), jnp.float32, 0.0, 100.0)
        edge_attr = jnp.concatenate([times, node_type[edge_index[0]][:, None].astype(jnp.float32), node_type[edge_index[1]][:, None].astype(jnp.float32)], axis=1)
        s = 0.02
        Wk = jax.random.normal(ks[4], (T, IN, PROJ), jnp.float32) * s
        Wq = jax.random.normal(ks[5], (T, IN, PROJ), jnp.float32) * s
        Wv = jax.random.normal(ks[6], (T, IN, PROJ), jnp.float32) * s
        bk = jnp.zeros((T, PROJ), jnp.float32)
        bq = jnp.zeros((T, PROJ), jnp.float32)
        bv = jnp.zeros((T, PROJ), jnp.float32)
        Wa = jax.random.normal(ks[7], (T, 2 * OUT, IN), jnp.float32) * s
        ba = jnp.zeros((T, IN), jnp.float32)
        gamma = jnp.ones((T, IN), jnp.float32)
        beta = jnp.zeros((T, IN), jnp.float32)
        w_time = jnp.asarray(1.0 / 10 ** np.linspace(0, 1.5, TD), jnp.float32)
        b_time = jnp.zeros((TD,), jnp.float32)
        return dict(x=x, node_type=node_type, edge_index=edge_index, edge_attr=edge_attr, Wk=Wk, bk=bk, Wq=Wq, bq=bq, Wv=Wv, bv=bv, Wa=Wa, ba=ba, gamma=gamma, beta=beta, w_time=w_time, b_time=b_time)
    _L0_gnn_all = _L0_gnn_setup()
    _L0_gnn_in = {k: v for k, v in _L0_gnn_all.items() if k in ('Wk', 'bk', 'Wq', 'bq', 'Wv', 'bv', 'Wa', 'ba', 'gamma', 'beta', 'w_time', 'b_time')}
    del _L0_gnn_all
    return {'x': x, 'src': src, 'dst': dst, 'edge_attr_5': edge_attr_5, 'node_type_19': node_type_19, 'L0_gnn_Wk': _L0_gnn_in['Wk'], 'L0_gnn_bk': _L0_gnn_in['bk'], 'L0_gnn_Wq': _L0_gnn_in['Wq'], 'L0_gnn_bq': _L0_gnn_in['bq'], 'L0_gnn_Wv': _L0_gnn_in['Wv'], 'L0_gnn_bv': _L0_gnn_in['bv'], 'L0_gnn_Wa': _L0_gnn_in['Wa'], 'L0_gnn_ba': _L0_gnn_in['ba'], 'L0_gnn_gamma': _L0_gnn_in['gamma'], 'L0_gnn_beta': _L0_gnn_in['beta'], 'L0_gnn_w_time': _L0_gnn_in['w_time'], 'L0_gnn_b_time': _L0_gnn_in['b_time']}

def reference(x, src, dst, edge_attr_5, node_type_19, L0_gnn_Wk, L0_gnn_bk, L0_gnn_Wq, L0_gnn_bq, L0_gnn_Wv, L0_gnn_bv, L0_gnn_Wa, L0_gnn_ba, L0_gnn_gamma, L0_gnn_beta, L0_gnn_w_time, L0_gnn_b_time):
    import jax
    import jax.numpy as jnp

    def _L0_gnn_ref(x, node_type, edge_index, edge_attr, Wk, bk, Wq, bq, Wv, bv, Wa, ba, gamma, beta, w_time, b_time):
        import jax, jax.numpy as jnp
        import numpy as np
        N = 4096
        E = 16384
        IN = 256
        OUT = 256
        TD = 32
        H = 4
        T = 19
        PROJ = OUT - 2 * TD
        DK = (OUT - TD) // H
        SQRT_DK = float(np.sqrt(DK))
        LN_EPS = 1e-05

        def time_emb(t, w, b):
            return jnp.cos(jnp.log(t + 1.0)[:, None] * w[None, :] + b[None, :])

        def typed_linear(x, W, b, node_type):
            out = jnp.zeros((x.shape[0], W.shape[2]), x.dtype)
            for t in range(W.shape[0]):
                out = jnp.where((node_type == t)[:, None], x @ W[t] + b[t], out)
            return out

        def seg_softmax(att, idx, n):
            m = jax.ops.segment_max(att, idx, num_segments=n)
            e = jnp.exp(att - m[idx])
            s = jax.ops.segment_sum(e, idx, num_segments=n)
            return e / (s[idx] + 1e-16)
        row, col = (edge_index[0], edge_index[1])
        n = x.shape[0]
        K = typed_linear(x, Wk, bk, node_type)
        Q = typed_linear(x, Wq, bq, node_type)
        V = typed_linear(x, Wv, bv, node_type)
        e0 = time_emb(edge_attr[:, 0], w_time, b_time)
        e1 = time_emb(edge_attr[:, 1], w_time, b_time)
        e2 = time_emb(edge_attr[:, 2], w_time, b_time)

        def edge_msgs(Kn, Qn, Vn, ek, eq):
            k = jnp.concatenate([Kn, ek], axis=1).reshape(-1, H, DK)
            q = jnp.concatenate([Qn, eq], axis=1).reshape(-1, H, DK)
            att = jnp.einsum('ehd,ed->eh', k, q.sum(axis=1)) / SQRT_DK
            v = jnp.concatenate([Vn, ek], axis=1).reshape(-1, H, DK)
            return (att, v)
        att, v = edge_msgs(K[row], Q[col], V[row], e1, e2)
        att_i, v_i = edge_msgs(K[col], Q[row], V[col], e2, e1)
        att = seg_softmax(att, col, n)
        att_i = seg_softmax(att_i, row, n)
        res = (v * att[:, :, None]).reshape(-1, H * DK)
        res = jnp.concatenate([res, e0], axis=1)
        res_i = (v_i * att_i[:, :, None]).reshape(-1, H * DK)
        res_i = jnp.concatenate([res_i, e0], axis=1)
        agg = jax.ops.segment_sum(res, col, num_segments=n) + jax.ops.segment_sum(res_i, row, num_segments=n)
        h = jnp.concatenate([agg, agg], axis=1)
        o = typed_linear(h, Wa, ba, node_type)
        y = o + x
        mu = y.mean(axis=-1, keepdims=True)
        var = y.var(axis=-1, keepdims=True)
        yn = (y - mu) / jnp.sqrt(var + LN_EPS)
        return yn * gamma[node_type] + beta[node_type]
    edge_index = jnp.stack([src, dst])
    x = _layernorm(x + _L0_gnn_ref(x, node_type_19, edge_index, edge_attr_5, L0_gnn_Wk, L0_gnn_bk, L0_gnn_Wq, L0_gnn_bq, L0_gnn_Wv, L0_gnn_bv, L0_gnn_Wa, L0_gnn_ba, L0_gnn_gamma, L0_gnn_beta, L0_gnn_w_time, L0_gnn_b_time), axis=-1)
    return x

_drawn_inputs = setup_inputs


def setup_inputs(seed=0):
    import zlib

    import numpy as np

    out = dict(_drawn_inputs(seed))
    spreads = {'L0_gnn_bk': (0.0, 0.8),
     'L0_gnn_bq': (0.0, 0.8),
     'L0_gnn_bv': (0.0, 0.8),
     'L0_gnn_ba': (0.0, 0.8),
     'L0_gnn_gamma': (1.0, 0.2),
     'L0_gnn_beta': (0.0, 0.1),
     'L0_gnn_b_time': (0.0, 0.1)}
    factors = {'L0_gnn_Wk': 8.0, 'L0_gnn_Wq': 8.0, 'L0_gnn_Wv': 8.0}
    for name, (base, spread) in spreads.items():
        noise = np.random.default_rng([zlib.crc32(name.encode()), seed]).standard_normal(out[name].shape)
        drawn = base * np.exp(spread * noise) if base else spread * noise
        out[name] = jnp.asarray(drawn.astype(out[name].dtype))
    for name, factor in factors.items():
        out[name] = (out[name] * factor).astype(out[name].dtype)
    return out
```

```python
import math
from contextlib import ExitStack

import numpy as np

import concourse.bass as bass
from concourse import mybir

F32 = mybir.dt.float32
BF16 = mybir.dt.bfloat16
I32 = mybir.dt.int32
ALU = mybir.AluOpType
ACT = mybir.ActivationFunctionType
AX = mybir.AxisListType.X

P = 128
MAGIC = 12582912.0
LOW = -1.0e38
PAD_LO = 128.0
LN_EPS = 1e-05


class Sizes:

    def __init__(self, x, dst, Wk, Wa, w_time):
        self.N, self.IN = x.shape
        self.E = dst.shape[0]
        self.T, _, self.PROJ = Wk.shape
        self.TD = w_time.shape[0]
        self.OUT = Wa.shape[1] // 2
        self.H = 4
        self.DK = (self.PROJ + self.TD) // self.H
        self.KC = self.IN // P
        self.NO = -(-self.N // P)
        self.LAST = self.N - (self.NO - 1) * P
        self.CE = self.E // P
        self.REST = self.E - self.CE * P
        self.SG = 16
        self.CT = -(-(self.CE + (self.REST > 0)) // (2 * self.SG)) * 2 * self.SG
        used = (self.E + self.NO * (P - 1)) // P
        self.G = 8
        self.NT = -(-used // (2 * self.G)) * 2 * self.G
        self.TP = -(-used // P)
        self.SP = -(-used // self.TP)
        self.NB = -(-max(self.NT, self.SP * self.TP) // 32)
        self.NT2 = self.NB * 32
        self.REC = 5
        self.VW = self.PROJ + 2 * self.TD
        self.ROW = 2 * self.PROJ + 2 * self.TD


def chain(eng, sem, base=0):
    n = [0]

    def link(ins):
        n[0] += 1
        ins.then_inc(sem, 1)
        eng.wait_ge(sem, base + n[0])

    return link, n


def bc(ap, axis, count):
    shape = list(ap.shape)
    shape.insert(axis, count)
    return ap.unsqueeze(axis).broadcast_to(shape)


class Scope:

    held = []

    def __init__(self, nc, ctx, tag):
        self.nc, self.ctx, self.tag = nc, ctx, tag

    def sb(self, name, shape, dt=F32):
        return self.ctx.enter_context(self.nc.sbuf_tensor(f"{self.tag}_{name}", shape, dt))

    def pb(self, name, shape=(P, 512), dt=F32):
        return self.ctx.enter_context(self.nc.psum_tensor(f"{self.tag}_{name}", list(shape), dt))

    def sem(self, name):
        self.held.append(self.nc.alloc_semaphore(f"{self.tag}_{name}"))
        return self.held[-1]

    @classmethod
    def retire(cls, nc):
        nc.clear_and_free_semaphores(cls.held)
        cls.held = []
        nc.all_engine_barrier()


def constants(nc, k, S):
    with ExitStack() as ctx:
        s = Scope(nc, ctx, "const")
        s_pool = s.sem("pool")
        s_dve = s.sem("dve")
        block = ctx.enter_context(nc.Block())

        @block.gpsimd
        def _(pool):
            link, _ = chain(pool, s_pool)
            link(nc.gpsimd.memset(k.ident[:], 0.0))
            link(nc.gpsimd.affine_select(out=k.ident[:], in_=k.ident[:], compare_op=ALU.not_equal, fill=1.0,
                                         base=0, pattern=[[-1, P]], channel_multiplier=1))
            link(nc.gpsimd.iota(k.ramp_i[:], pattern=[[1, P]], base=0, channel_multiplier=0))

        @block.vector
        def _(dve):
            link, _ = chain(dve, s_dve)
            dve.wait_ge(s_pool, 3)
            link(nc.vector.tensor_copy(k.ident_b[:], k.ident[:]))
            link(nc.vector.tensor_copy(k.ramp[:], k.ramp_i[:]))
            link(nc.vector.tensor_copy(k.ramp16[:], bc(k.ramp[:], 2, 16)))


def project(nc, k, S, x, ntype, Wk, bk, Wq, bq, Wv, bv, table):
    H, DK, PROJ, T, KC = S.H, S.DK, S.PROJ, S.T, S.KC
    TAIL = PROJ - (H - 1) * DK
    WN = 2 * PROJ + DK
    with ExitStack() as ctx:
        s = Scope(nc, ctx, "proj")
        W = s.sb("W", [P, KC, T, WN])
        Wqr = s.sb("Wqr", [P, KC, T, PROJ])
        B = s.sb("B", [T, WN])
        Bqr = s.sb("Bqr", [T, PROJ])
        tid_i = s.sb("tid_i", [T, 1], I32)
        tid = s.sb("tid", [T, 1])
        xr = s.sb("xr", [P, 2, S.IN])
        ty = s.sb("ty", [P, 2, P], I32)
        xT = s.sb("xT", [P, KC, P])
        xm = s.sb("xm", [P, T, KC, P])
        oneT = s.sb("oneT", [T, P])
        kv = s.sb("kv", [P, 2 * PROJ])
        pT = s.pb("pT")
        pP = s.pb("pP")
        s_w, s_id, s_wq, s_x, s_xT, s_xTc, s_m, s_p, s_pc, s_kv, s_free = [
            s.sem(n) for n in ("w", "id", "wq", "x", "xT", "xTc", "m", "p", "pc", "kv", "free")]
        s_dve = s.sem("dve")
        block = ctx.enter_context(nc.Block())
        full = S.NO - 1

        @block.sync
        def _(sp):
            for c in range(KC):
                r = slice(c * P, (c + 1) * P)
                sp.dma_start(W[:, c, :, 0:PROJ], Wv[:, r, :].rearrange("t p n -> p t n")).then_inc(s_w, 16)
                sp.dma_start(W[:, c, :, PROJ:2 * PROJ], Wk[:, r, :].rearrange("t p n -> p t n")).then_inc(s_w, 16)
                sp.dma_start(Wqr[:, c, :, :], Wq[:, r, :].rearrange("t p n -> p t n")).then_inc(s_w, 16)
            sp.dma_start(B[:, 0:PROJ], bv).then_inc(s_w, 16)
            sp.dma_start(B[:, PROJ:2 * PROJ], bk).then_inc(s_w, 16)
            sp.dma_start(Bqr[:], bq).then_inc(s_w, 16)

            def load(o, rows, n):
                sp.wait_ge(s_p, n)
                sp.dma_start(xr[0:rows, 0, :], x[bass.ds(o * P, rows), :]).then_inc(s_x, 16)
                sp.dma_start(ty[:, 0, 0:rows], bc(ntype[bass.ds(o * P, rows)], 0, P)).then_inc(s_x, 16)
                sp.wait_ge(s_pc, n + 1)
                sp.dma_start(table[bass.ds(o * P, rows), :], kv[0:rows, :]).then_inc(s_kv, 16)

            if full:
                with sp.Fori(0, full) as o:
                    load(o, P, o)
            load(full, S.LAST, full)
            sp.wait_ge(s_kv, 16 * S.NO)

        @block.gpsimd
        def _(pool):
            nc.gpsimd.iota(tid_i[:], pattern=[[0, 1]], base=0, channel_multiplier=1).then_inc(s_id, 1)

        @block.vector
        def _(dve):
            link, _ = chain(dve, s_dve)
            dve.wait_ge(s_w, 16 * (3 * KC + 3))
            dve.wait_ge(s_id, 1)
            nc.vector.tensor_copy(tid[:], tid_i[:])
            for dst_, src_ in ((W, Wqr), (B, Bqr)):
                lead = [slice(None)] * (len(src_.shape) - 1)

                def q(a, b):
                    return src_[tuple(lead + [slice(a, b)])]

                def o(a, b):
                    return dst_[tuple(lead + [slice(2 * PROJ + a, 2 * PROJ + b)])]

                link(nc.vector.tensor_tensor(o(0, DK), q(0, DK), q(DK, 2 * DK), ALU.add))
                link(nc.vector.tensor_tensor(o(0, DK), o(0, DK), q(2 * DK, 3 * DK), ALU.add))
                link(nc.vector.tensor_tensor(o(0, TAIL), o(0, TAIL), q(3 * DK, PROJ), ALU.add))
            nc.vector.memset(k.qs[:, full * DK:(full + 1) * DK], 0.0).then_inc(s_wq, 1)

            def tile(rows, n):
                dve.wait_ge(s_x, 32 * (n + 1))
                dve.wait_ge(s_p, n)
                nc.vector.tensor_scalar(oneT[:, 0:rows], ty[0:T, 0, 0:rows], tid[:, 0:1], None, ALU.is_equal)
                dve.wait_ge(s_xTc, n + 1)
                for t in range(T):
                    nc.vector.scalar_tensor_tensor(out=xm[:, t, :, 0:rows], in0=bc(ty[:, 0, 0:rows], 1, KC), scalar=float(t),
                                                   in1=xT[:, :, 0:rows], op0=ALU.is_equal, op1=ALU.mult).then_inc(s_m, 1)

            if full:
                with dve.Fori(0, full) as o:
                    tile(P, o)
            tile(S.LAST, full)

        @block.tensor
        def _(pe):
            pe.wait_ge(s_wq, 1)

            def tile(rows, n):
                pe.wait_ge(s_x, 32 * (n + 1))
                pe.wait_ge(s_xTc, n)
                for c in range(KC):
                    last = nc.tensor.transpose(pT[:, c * P:c * P + rows], xr[0:rows, 0, c * P:(c + 1) * P], k.ident[0:rows, 0:rows])
                last.then_inc(s_xT, 1)
                pe.wait_ge(s_pc, n)
                for t in range(T):
                    pe.wait_ge(s_m, n * T + t + 1)
                    for c in range(KC):
                        nc.tensor.matmul(pP[0:rows, 0:WN], xm[:, t, c, 0:rows], W[:, c, t, :], start=(t == 0 and c == 0), stop=False)
                nc.tensor.matmul(pP[0:rows, 0:WN], oneT[:, 0:rows], B[:], start=False, stop=True).then_inc(s_p, 1)

            if full:
                with pe.Fori(0, full) as o:
                    tile(P, o)
            tile(S.LAST, full)

        @block.scalar
        def _(act):
            def tile(o, rows, n):
                act.wait_ge(s_xT, n + 1)
                nc.scalar.activation(xT[:, :, 0:rows], pT[:, 0:KC * P].rearrange("p (c n) -> p c n", c=KC)[:, :, 0:rows], ACT.Copy).then_inc(s_xTc, 1)
                act.wait_ge(s_p, n + 1)
                act.wait_ge(s_kv, 16 * n)
                nc.scalar.activation(k.qs[0:rows, bass.ds(o * DK, DK)], pP[0:rows, 2 * PROJ:WN], ACT.Copy)
                nc.scalar.activation(kv[0:rows, :], pP[0:rows, 0:2 * PROJ], ACT.Copy).then_inc(s_pc, 1)

            act.wait_ge(s_wq, 1)
            if full:
                with act.Fori(0, full) as o:
                    tile(o, P, o)
            tile(full, S.LAST, full)


def one_hots(nc, S, k, oh_lo, oh_hi, piece, ramp_hi, par, col):
    for d in range(2):
        nc.vector.tensor_tensor(oh_lo[:, par, d], bc(piece[:, d, 0, bass.ds(col, S.SG)], 1, P), k.ramp16[:], ALU.is_equal)
        last = nc.vector.tensor_tensor(oh_hi[:, par, d], bc(piece[:, d, 1, bass.ds(col, S.SG)], 1, S.NO), ramp_hi[:], ALU.is_equal)
    return last


def sort_edges(nc, k, S, src, dst, edge_attr, recs):
    CT, CE, REST, SG, NO, NT, REC = S.CT, S.CE, S.REST, S.SG, S.NO, S.NT, S.REC
    NG = CT // SG
    with ExitStack() as ctx:
        s = Scope(nc, ctx, "sort")
        raw = s.sb("raw", [P, 2, CT], I32)
        own = s.sb("own", [P, 2, CT])
        piece = s.sb("piece", [P, 2, 2, CT], BF16)
        ea = s.sb("ea", [P, CT, 5])
        inval = s.sb("inval", [P, CT])
        ramp_hi = s.sb("ramp_hi", [P, NO, SG], BF16)
        oh_lo = s.sb("oh_lo", [P, 2, 2, P, SG], BF16)
        oh_hi = s.sb("oh_hi", [P, 2, 2, NO, SG], BF16)
        tri = s.sb("tri", [P, P])
        sel = s.sb("sel", [64, 32, P], BF16)
        base = s.sb("base", [P, 2, NO])
        count_owners(nc, k, S, src, dst, edge_attr, recs, raw, own, piece, ea, inval, ramp_hi, oh_lo, oh_hi, tri, sel, base)
        place_edges(nc, k, S, recs, raw, own, piece, ea, inval, ramp_hi, oh_lo, oh_hi, tri, sel, base)


def count_owners(nc, k, S, src, dst, edge_attr, recs, raw, own, piece, ea, inval, ramp_hi, oh_lo, oh_hi, tri, sel, base):
    CT, CE, REST, SG, NO, NT, REC = S.CT, S.CE, S.REST, S.SG, S.NO, S.NT, S.REC
    NG = CT // SG
    TC = -(-NT // 4)
    assert TC <= 512
    with ExitStack() as ctx:
        s = Scope(nc, ctx, "count")
        tmp = s.sb("tmp", [P, 2, CT], I32)
        padrec = s.sb("padrec", [P, NT // 8, REC])
        triT = s.sb("triT", [P, P])
        ones = s.sb("ones", [P, P])
        zero = s.sb("zero", [P, P])
        hs = s.sb("hs", [P, 2, NO])
        st = s.sb("st", [P, 4, NO])
        sti = s.sb("sti", [P, NO], I32)
        stc = s.sb("stc", [P, 2])
        ramp_ti = s.sb("ramp_ti", [NO, NT], I32)
        ge = s.sb("ge", [NO, NT])
        junk = s.sb("junk", [P, NO])
        pH = [s.pb(f"pH{d}") for d in range(2)]
        pO = [s.pb(f"pO{n}") for n in range(4)]
        s_in, s_ea, s_dve, s_c, s_oh, s_h, s_hc, s_o, s_oc, s_ot, s_pad, s_prep = [
            s.sem(n) for n in ("in", "ea", "dve", "c", "oh", "h", "hc", "o", "oc", "ot", "pad", "prep")]
        block = ctx.enter_context(nc.Block())

        @block.sync
        def _(sp):
            sp.wait_ge(s_c, 1)
            for d, a in enumerate((dst, src)):
                sp.dma_start(raw[:, d, 0:CE], a[0:CE * P].rearrange("(p c) -> p c", p=P)).then_inc(s_in, 16)
                if REST:
                    sp.dma_start(raw[0:REST, d, CE:CE + 1], a[CE * P:].unsqueeze(1)).then_inc(s_in, 16)
            sp.wait_ge(s_c, 2)
            sp.dma_start(ea[:, 0:CE, :], edge_attr[0:CE * P, :].rearrange("(p c) f -> p c f", p=P)).then_inc(s_ea, 16)
            if REST:
                sp.dma_start(ea[0:REST, CE, :], edge_attr[CE * P:, :]).then_inc(s_ea, 16)
            sp.wait_ge(s_c, 3)
            for d in range(2):
                r = recs[d].rearrange("(p c) f -> p c f", p=P)
                for n in range(8):
                    w = NT // 8
                    sp.dma_start(r[:, n * w:(n + 1) * w, :], padrec[:]).then_inc(s_pad, 16)
            sp.wait_ge(s_pad, 256)
            sp.wait_ge(s_ea, 32 if REST else 16)

        @block.gpsimd
        def _(pool):
            link, _ = chain(pool, s_prep)
            link(nc.gpsimd.iota(ramp_ti[:], pattern=[[1, NT]], base=0, channel_multiplier=0))
            link(nc.gpsimd.memset(ones[:], 1.0))
            link(nc.gpsimd.affine_select(out=triT[:], in_=ones[:], compare_op=ALU.is_gt, fill=0.0,
                                         base=0, pattern=[[1, P]], channel_multiplier=-1))
            link(nc.gpsimd.affine_select(out=tri[:], in_=ones[:], compare_op=ALU.is_gt, fill=0.0,
                                         base=0, pattern=[[-1, P]], channel_multiplier=1))
            link(nc.gpsimd.memset(sel[:], 0.0))
            v = sel[:].rearrange("r (d k) m -> r d k m", d=2)
            for off in (0, 16):
                for d in range(2):
                    link(nc.gpsimd.affine_select(out=v[:, d], in_=v[:, d], compare_op=ALU.not_equal, fill=1.0,
                                                 base=-off - 32 * d, pattern=[[-1, 16], [0, P]], channel_multiplier=1))

        @block.vector
        def _(dve):
            link, _ = chain(dve, s_dve)
            nc.vector.memset(raw[:, :, CE:CT], 100 * P).then_inc(s_c, 1)
            nc.vector.memset(ea[:, CE:CT, :], 0.0).then_inc(s_c, 1)
            link(nc.vector.memset(padrec[:], 0.0))
            nc.vector.memset(padrec[:, :, 3:4], -1.0).then_inc(s_c, 1)
            nc.vector.memset(zero[:], 0.0).then_inc(s_c, 1)
            link(nc.vector.tensor_scalar(st[:, 0, :], k.ramp[:, 0:NO], float(P), None, ALU.mult))
            link(nc.vector.tensor_copy(ramp_hi[:], bc(st[:, 0, :], 2, SG)))
            dve.wait_ge(s_in, 64 if REST else 32)
            link(nc.vector.tensor_copy(own[:], raw[:]))
            link(nc.vector.tensor_scalar(tmp[:], raw[:], P - 1, None, ALU.bitwise_and))
            link(nc.vector.tensor_copy(piece[:, :, 0, :], tmp[:]))
            link(nc.vector.tensor_tensor(piece[:, :, 1, :], own[:], tmp[:], ALU.subtract))
            link(nc.vector.tensor_scalar(inval[:], own[:, 0, :], 100.0 * P, float(1 << 20), ALU.is_ge, ALU.mult))
            with dve.Fori(0, NG // 2) as i:
                for par in range(2):
                    dve.wait_ge(s_h, 2 * i + par)
                    one_hots(nc, S, k, oh_lo, oh_hi, piece, ramp_hi, par, (2 * i + par) * SG).then_inc(s_oh, 1)
            dve.wait_ge(s_h, NG + 1)
            nc.vector.tensor_copy(hs[:, 0, :], pH[0][:, 0:NO])
            link(nc.vector.tensor_copy(hs[:, 1, :], pH[1][:, 0:NO]))
            nc.vector.tensor_copy(junk[:], pH[1][:, 0:NO]).then_inc(s_hc, 1)
            for d in range(2):
                dve.wait_ge(s_o, d + 1)
                link(nc.vector.tensor_scalar(sti[:], pO[1][:, 0:NO], float(P - 1), None, ALU.add))
                link(nc.vector.tensor_scalar(sti[:], sti[:], 7, None, ALU.logical_shift_right))
                link(nc.vector.tensor_copy(st[:, 1, :], sti[:]))
                link(nc.vector.tensor_tensor_scan(st[:, 2, :], st[:, 1, :], zero[:, 0:NO], 0.0, ALU.add, ALU.add))
                link(nc.vector.tensor_tensor(st[:, 3, :], st[:, 2, :], st[:, 1, :], ALU.subtract))
                link(nc.vector.scalar_tensor_tensor(out=base[:, d, :], in0=st[:, 3, :], scalar=float(P), in1=pO[0][:, 0:NO],
                                                    op0=ALU.mult, op1=ALU.add))
                link(nc.vector.tensor_tensor(junk[:], st[:, 3, :], k.ident[:, 0:NO], ALU.mult))
                link(nc.vector.tensor_reduce(stc[:, d:d + 1], junk[:], op=ALU.add, axis=AX))
                dve.wait_ge(s_prep, 1)
                nc.vector.tensor_scalar(ge[:], ramp_ti[:], stc[0:NO, d:d + 1], None, ALU.is_ge).then_inc(s_oc, 1)
                dve.wait_ge(s_ot, d + 1)
                for n in range(4):
                    w = min(TC, NT - n * TC)
                    last = nc.vector.tensor_scalar(k.otile[d][0:1, n * TC:n * TC + w], pO[n][0:1, 0:w], -1.0, None, ALU.add)
                last.then_inc(s_hc, 1)

        @block.tensor
        def _(pe):
            pe.wait_ge(s_c, 4)
            nc.tensor.matmul(pH[0][:, 0:NO], zero[:], zero[:, 0:NO], start=True, stop=True)
            nc.tensor.matmul(pH[1][:, 0:NO], zero[:], zero[:, 0:NO], start=True, stop=True).then_inc(s_h, 1)
            with pe.Fori(0, NG // 2) as i:
                for par in range(2):
                    pe.wait_ge(s_oh, 2 * i + par + 1)
                    for d in range(2):
                        for t in range(SG):
                            last = nc.tensor.matmul(pH[d][:, 0:NO], oh_lo[:, par, d, :, t], oh_hi[:, par, d, :, t],
                                                    start=False, stop=True, skip_group_check=True)
                    last.then_inc(s_h, 1)
            pe.wait_ge(s_prep, 4)
            for d in range(2):
                pe.wait_ge(s_hc, d + 1)
                nc.tensor.matmul(pO[0][:, 0:NO], triT[:], hs[:, d, :], start=True, stop=True)
                nc.tensor.matmul(pO[1][:, 0:NO], ones[:], hs[:, d, :], start=True, stop=True).then_inc(s_o, 1)
                pe.wait_ge(s_oc, d + 1)
                for n in range(4):
                    w = min(TC, NT - n * TC)
                    last = nc.tensor.matmul(pO[n][0:1, 0:w], ones[0:NO, 0:1], ge[:, n * TC:n * TC + w], start=True, stop=True)
                last.then_inc(s_ot, 1)


def place_edges(nc, k, S, recs, raw, own, piece, ea, inval, ramp_hi, oh_lo, oh_hi, tri, sel, base):
    CT, SG, NO, NT, REC = S.CT, S.SG, S.NO, S.NT, S.REC
    NG, Q = CT // SG, S.SG // 4
    with ExitStack() as ctx:
        s = Scope(nc, ctx, "place")
        own_g = s.sb("own_g", [P, 2, 2, SG])
        piece_g = s.sb("piece_g", [P, 2, P], BF16)
        rec = s.sb("rec", [P, 2, 2, SG, REC])
        rows = s.sb("rows", [64, P], BF16)
        t_lo = s.sb("t_lo", [P, 8, P])
        cur = s.sb("cur", [P, 2, NO])
        junk = s.sb("junk", [P, 2, 4, P], BF16)
        prod = s.sb("prod", [P, 2, 8, NO])
        mark = s.sb("mark", [P, 2])
        below = s.sb("below", [P, 2, 2, SG])
        found = s.sb("found", [P, 2, 2, SG])
        slot = s.sb("slot", [P, 2, SG])
        slot_i = s.sb("slot_i", [P, 2, SG], I32)
        slot_l = s.sb("slot_l", [P, 2, SG], I32)
        addr = s.sb("addr", [P, 2, 2, SG], I32)
        pC = [s.pb(f"pC{d}") for d in range(2)]
        pT = s.pb("pT", [P, 8, P], BF16)
        pB = [s.pb(f"pB{d}", [P, 4, P]) for d in range(2)]
        pL = [s.pb(f"pL{n}") for n in range(2)]
        s_stage, s_oh, s_rowp, s_rows, s_tps, s_tlo, s_l, s_selr, s_addr, s_link, s_ohf = [
            s.sem(n) for n in ("stage", "oh", "rowp", "rows", "tps", "tlo", "l", "selr", "addr", "link", "ohf")]
        s_b, s_eq, s_cnt, s_cur = [[s.sem(f"{n}{d}") for d in range(2)] for n in ("b", "eq", "cnt", "cur")]
        s_turn = s.sem("turn")
        s_scat = [s.sem(f"scat{p}") for p in range(2)]
        block = ctx.enter_context(nc.Block())

        @block.scalar
        def _(act):
            act.wait_ge(s_addr, 1)
            for d in range(2):
                act.wait_ge(s_cnt[d], 1)
                nc.scalar.activation(cur[:, d, :], pC[d][:, 0:NO], ACT.Copy).then_inc(s_cur[d], 1)
            with act.Fori(0, NG // 2) as i:
                for par in range(2):
                    g = 2 * i + par
                    act.wait_ge(s_addr, g)
                    act.wait_ge(s_scat[par], i * (32 * SG))
                    act.wait_ge(s_rowp, g)
                    nc.scalar.activation(own_g[:, par], own[:, :, bass.ds(g * SG, SG)], ACT.Copy)
                    nc.scalar.activation(piece_g[:, par, 0:4 * SG].rearrange("p (d a t) -> p d a t", d=2, a=2), piece[:, :, :, bass.ds(g * SG, SG)], ACT.Copy).then_inc(s_stage, 1)
                    for d in range(2):
                        e = ea[:, bass.ds(g * SG, SG), :]
                        r = rec[:, par, d]
                        nc.scalar.activation(r[:, :, 0:1], e[:, :, 0:1], ACT.Copy)
                        nc.scalar.activation(r[:, :, 1:2], e[:, :, 1 + d:2 + d], ACT.Copy)
                        nc.scalar.activation(r[:, :, 2:3], e[:, :, 2 - d:3 - d], ACT.Copy)
                        nc.scalar.activation(r[:, :, 3:4], own[:, d, bass.ds(g * SG, SG)].unsqueeze(2), ACT.Copy)
                        last = nc.scalar.activation(r[:, :, 4:5].bitcast(I32), raw[:, 1 - d, bass.ds(g * SG, SG)].unsqueeze(2), ACT.Copy)
                    last.then_inc(s_stage, 1)
                    act.wait_ge(s_rowp, g + 1)
                    nc.scalar.activation(rows[:], pT[0:64, 0, :], ACT.Copy).then_inc(s_rows, 1)
                    for q in range(Q):
                        n = Q * g + q
                        act.wait_ge(s_tps, n + 1)
                        nc.scalar.activation(t_lo[:], pT[:], ACT.Copy).then_inc(s_tlo, 1)
                        for t in range(4):
                            for d in range(2):
                                act.wait_ge(s_cnt[d], 4 * n + t + 2)
                                nc.scalar.activation(cur[:, d, :], pC[d][:, 0:NO], ACT.Copy).then_inc(s_cur[d], 1)

        @block.tensor
        def _(pe):
            for d in range(2):
                nc.tensor.matmul(pC[d][:, 0:NO], k.ident[:], base[:, d, :], start=True, stop=True).then_inc(s_cnt[d], 1)
            with pe.Fori(0, NG // 2) as i:
                for par in range(2):
                    g = 2 * i + par
                    pe.wait_ge(s_stage, 2 * g + 1)
                    pe.wait_ge(s_tlo, Q * g)
                    nc.tensor.transpose(pT[:, 0, :], piece_g[:, par, :], k.ident_b[:]).then_inc(s_rowp, 1)
                    pe.wait_ge(s_rows, g + 1)
                    pe.wait_ge(s_oh, g + 1)
                    for q in range(Q):
                        n = Q * g + q
                        for d in range(2):
                            pe.wait_ge(s_eq[d], n)
                            for t in range(4):
                                last = nc.tensor.matmul(pB[d][:, t, :], sel[:, d * 16 + 4 * q + t, :], rows[:], start=True, stop=True)
                            last.then_inc(s_b[d], 1)
                        pe.wait_ge(s_tlo, n)
                        for t in range(4):
                            for d in range(2):
                                last = nc.tensor.transpose(pT[:, 2 * t + d, :], oh_lo[:, par, d, :, 4 * q + t], k.ident_b[:])
                        last.then_inc(s_tps, 1)
                        pe.wait_ge(s_tlo, n + 1)
                        pe.wait_ge(s_selr, n)
                        for t in range(4):
                            for d in range(2):
                                j = 2 * t + d
                                pe.wait_ge(s_cur[d], 4 * n + t + 1)
                                last = nc.tensor.matmul(pL[q % 2][:, j * NO:(j + 1) * NO], t_lo[:, j, :], cur[:, d, :], start=True, stop=True)
                                nc.tensor.matmul(pC[d][:, 0:NO], oh_lo[:, par, d, :, 4 * q + t], oh_hi[:, par, d, :, 4 * q + t],
                                                 start=False, stop=True, skip_group_check=True).then_inc(s_cnt[d], 1)
                        last.then_inc(s_l, 1)

        @block.vector
        def _(dve):
            nc.vector.memset(piece_g[:], 0.0).then_inc(s_addr, 1)
            nc.vector.memset(slot[:], 0.0).then_inc(s_selr, 1)
            PER = 2 * 5
            with dve.Fori(0, NG // 2) as i:
                link, n_link = chain(dve, s_link, i * PER)
                for par in range(2):
                    g = 2 * i + par
                    dve.wait_ge(s_l, Q * g)
                    one_hots(nc, S, k, oh_lo, oh_hi, piece, ramp_hi, par, g * SG).then_inc(s_oh, 1)
                    dve.wait_ge(s_stage, 2 * g + 1)
                    for q in range(Q):
                        n = Q * g + q
                        for d in range(2):
                            dve.wait_ge(s_b[d], n + 1)
                            for t in range(4):
                                c = 4 * q + t
                                last = nc.vector.scalar_tensor_tensor(
                                    out=junk[:, d, t, :], in0=pB[d][:, t, :], scalar=own_g[:, par, d, c:c + 1], in1=tri[:],
                                    op0=ALU.is_equal, op1=ALU.mult, accum_out=below[:, par, d, c:c + 1])
                            last.then_inc(s_eq[d], 1)
                        dve.wait_ge(s_l, n + 1)
                        nc.vector.tensor_tensor(prod[:, q % 2].rearrange("p (t d) o -> p t d o", d=2),
                                                pL[q % 2][:, 0:8 * NO].rearrange("p (t d o) -> p t d o", t=4, d=2),
                                                oh_hi[:, par, :, :, 4 * q:4 * q + 4].rearrange("p d o t -> p t d o"),
                                                ALU.mult).then_inc(s_selr, 1)
                        dve.wait_ge(s_selr, n + 2)
                        last = nc.vector.tensor_reduce(found[:, par, :, 4 * q:4 * q + 4].rearrange("p d t -> p t d"),
                                                       prod[:, q % 2].rearrange("p (t d) o -> p t d o", d=2), op=ALU.add, axis=AX)
                    link(last)
                    link(nc.vector.tensor_tensor(slot_i[:], below[:, par], found[:, par], ALU.add))
                    nc.vector.tensor_scalar(slot_l[:], slot_i[:], P - 1, None, ALU.bitwise_and)
                    link(nc.vector.tensor_scalar(slot_i[:], slot_i[:], 7, None, ALU.logical_shift_right))
                    link(nc.vector.scalar_tensor_tensor(out=slot[:], in0=slot_l[:], scalar=float(NT), in1=slot_i[:], op0=ALU.mult, op1=ALU.add))
                    dve.wait_ge(s_scat[par], i * (32 * SG))
                    link(nc.vector.tensor_tensor(addr[:, par], slot[:], bc(inval[:, bass.ds(g * SG, SG)], 1, 2), ALU.add))
                    nc.vector.tensor_copy(mark[:, par:par + 1], addr[:, par, 0, 0:1]).then_inc(s_addr, 1)
                assert n_link[0] == PER, n_link

        @block.gpsimd
        def _(pool):
            with pool.Fori(0, NG // 2) as i:
                for par in range(2):
                    pool.wait_ge(s_stage, 4 * i + 2 * par + 2)
                    pool.wait_ge(s_addr, 2 * i + par + 2)
                    pool.sem_inc(s_turn, 1)
                    for d in range(2):
                        for t in range(SG):
                            nc.gpsimd.indirect_dma_start(recs[d], bass.IndirectOffsetOnAxis(addr[:, par, d, t:t + 1], 0),
                                                         rec[:, par, d, t, :], None, bounds_check=P * NT - 1,
                                                         oob_is_err=False).then_inc(s_scat[par], 16)
            for par in range(2):
                pool.wait_ge(s_scat[par], (NG // 2) * 32 * SG)


def gather(nc, k, S, d, rec_d, table, spill, keys, att_d, w_time, b_time):
    NT, G, DK, PROJ, TD, H, REC, VW, ROW, NB = S.NT, S.G, S.DK, S.PROJ, S.TD, S.H, S.REC, S.VW, S.ROW, S.NB
    F3 = 3 * TD
    HF = G // 2 * F3
    QC = DK - TD
    with ExitStack() as ctx:
        s = Scope(nc, ctx, f"gather{d}")
        rec = s.sb("rec", [P, NT, REC])
        lo_i = s.sb("lo_i", [P, NT], I32)
        att = s.sb("att", [P, NB * 32, H])
        blk = s.sb("blk", [G * REC, G * F3])
        wb = s.sb("wb", [1, 2 * TD])
        bq = s.sb("bq", [1, F3])
        key = s.sb("key", [P, NB * 32])
        keyT = s.sb("keyT", [P, -(-NB * 32 // P), P])
        attT = s.sb("attT", [P, 2, 4, P])
        pT = s.pb("pT", [P, 4, P])
        with ExitStack() as ctx2:
            prepare(nc, k, S, Scope(nc, ctx2, f"prep{d}"), d, rec_d, keys, w_time, b_time, rec, lo_i, blk, wb, bq, key, keyT, att, pT)
        with ExitStack() as ctx2:
            scores(nc, k, S, Scope(nc, ctx2, f"score{d}"), d, table, spill, rec, blk, att)
        with ExitStack() as ctx2:
            s3 = Scope(nc, ctx2, f"att{d}")
            s_t, s_c, s_o = s3.sem("t"), s3.sem("c"), s3.sem("o")
            pA = [s3.pb(f"pA{n}", [P, 4, P]) for n in range(2)]
            block = ctx2.enter_context(nc.Block())
            loads = [list(range(b, min(b + 4, NB))) for b in range(0, NB, 4)]

            @block.tensor
            def _(pe):
                for n, bs in enumerate(loads):
                    if n >= 2:
                        pe.wait_ge(s_c, n - 1)
                    for j, b in enumerate(bs):
                        last = nc.tensor.transpose(pA[n % 2][:, j, :], att[:, b * 32:(b + 1) * 32, :].rearrange("p t h -> p (t h)"), k.ident[:])
                    last.then_inc(s_t, 1)

            @block.scalar
            def _(act):
                for n, bs in enumerate(loads):
                    act.wait_ge(s_t, n + 1)
                    if n >= 2:
                        act.wait_ge(s_o, 16 * (n - 1))
                    nc.scalar.activation(attT[:, n % 2, 0:len(bs), :], pA[n % 2][:, 0:len(bs), :], ACT.Copy).then_inc(s_c, 1)

            @block.sync
            def _(sp):
                v = att_d.rearrange("(b t) h e -> (t h) b e", t=32)
                for n, bs in enumerate(loads):
                    sp.wait_ge(s_c, n + 1)
                    if n:
                        sp.wait_ge(s_o, 16 * n)
                    sp.dma_start(v[:, bs[0]:bs[0] + len(bs), :], attT[:, n % 2, 0:len(bs), :]).then_inc(s_o, 16)
                sp.wait_ge(s_o, 16 * len(loads))


def prepare(nc, k, S, s, d, rec_d, keys, w_time, b_time, rec, lo_i, blk, wb, bq, key, keyT, att, pT):
    NT, G, TD, REC, NB = S.NT, S.G, S.TD, S.REC, S.NB
    F3 = 3 * TD
    NK = NB * 32 // P + (NB * 32 % P > 0)
    s_r, s_w, s_dve, s_blk, s_key, s_act, s_t, s_c, s_ko = [s.sem(n) for n in ("r", "w", "dve", "blk", "key", "act", "t", "c", "ko")]
    block = s.ctx.enter_context(nc.Block())

    @block.sync
    def _(sp):
        sp.dma_start(rec[:], rec_d.rearrange("(p c) f -> p c f", p=P)).then_inc(s_r, 16)
        sp.dma_start(wb[:, 0:TD], w_time.unsqueeze(0)).then_inc(s_w, 16)
        sp.dma_start(wb[:, TD:2 * TD], b_time.unsqueeze(0)).then_inc(s_w, 16)
        sp.wait_ge(s_blk, 1)
        for t in range(G):
            for word, col in ((0, 1), (1, 0), (2, 2)):
                sp.dma_start(blk[t * REC + word:t * REC + word + 1, t * F3 + col * TD:t * F3 + (col + 1) * TD], wb[:, 0:TD]).then_inc(s_w, 16)
            sp.dma_start(blk[t * REC + 3:t * REC + 4, t * F3:(t + 1) * F3], bq[:]).then_inc(s_w, 16)
        for n in range(NK):
            w = min(P, NB * 32 - n * P)
            sp.wait_ge(s_c, n + 1)
            sp.dma_start(keys[n * P:n * P + w, :], keyT[0:w, n, :]).then_inc(s_ko, 16)
        sp.wait_ge(s_ko, 16 * NK)
        sp.wait_ge(s_w, 32 + 64 * G)

    @block.vector
    def _(dve):
        link, _ = chain(dve, s_dve)
        link(nc.vector.memset(blk[:], 0.0))
        dve.wait_ge(s_w, 32)
        link(nc.vector.tensor_scalar(wb[:, 0:2 * TD], wb[:, 0:2 * TD], 1.0 / (2 * math.pi), None, ALU.mult))
        nc.vector.tensor_scalar(bq[:].rearrange("p (a b) -> p a b", a=3), bc(wb[:, TD:2 * TD], 1, 3), 0.25, None, ALU.add).then_inc(s_blk, 1)
        link(nc.vector.memset(key[:], -1.0))
        nc.vector.memset(att[:], 0.0)
        dve.wait_ge(s_r, 16)
        link(nc.vector.tensor_copy(key[:, 0:NT], rec[:, :, 3]))
        nc.vector.tensor_scalar(rec[:, :, 3], rec[:, :, 3], 0.0, 1.0, ALU.mult, ALU.add).then_inc(s_key, 1)
        link(nc.vector.tensor_copy(lo_i[:], key[:, 0:NT]))
        link(nc.vector.tensor_scalar(lo_i[:], lo_i[:], P - 1, None, ALU.bitwise_and))
        link(nc.vector.tensor_scalar(k.lo[d][:], key[:, 0:NT], 0.0, PAD_LO, ALU.is_lt, ALU.mult))
        link(nc.vector.tensor_tensor(k.lo[d][:], k.lo[d][:], lo_i[:], ALU.add))

    @block.tensor
    def _(pe):
        pe.wait_ge(s_key, 1)
        for n in range(NK):
            w = min(P, NB * 32 - n * P)
            if n:
                pe.wait_ge(s_c, n)
            nc.tensor.transpose(pT[0:w, 0, :], key[:, n * P:n * P + w], k.ident[:]).then_inc(s_t, 1)

    @block.scalar
    def _(act):
        act.wait_ge(s_r, 16)
        act.wait_ge(s_key, 1)
        nc.scalar.activation(rec[:, :, 0:3], rec[:, :, 0:3], ACT.Ln, bias=1.0).then_inc(s_act, 1)
        for n in range(NK):
            w = min(P, NB * 32 - n * P)
            act.wait_ge(s_t, n + 1)
            nc.scalar.activation(keyT[0:w, n, :], pT[0:w, 0, :], ACT.Copy).then_inc(s_c, 1)


def scores(nc, k, S, s, d, table, spill, rec, blk, att):
    NT, G, DK, PROJ, TD, H, REC, VW, ROW = S.NT, S.G, S.DK, S.PROJ, S.TD, S.H, S.REC, S.VW, S.ROW
    F3 = 3 * TD
    HG = G // 2
    QC = DK - TD
    NI = NT // (2 * G)
    row = [s.sb(f"row{n}", [P, G, ROW]) for n in range(2)]
    eq = [s.sb(f"eq{n}", [P, G, TD]) for n in range(2)]
    idx = [s.sb(f"idx{n}", [P, G], I32) for n in range(2)]
    logs = [s.sb(f"logs{n}", [P, P]) for n in range(2)]
    logT = [s.sb(f"logT{n}", [G * REC, P]) for n in range(2)]
    turns = s.sb("turns", [P, 2, HG, F3])
    frac = [s.sb(f"frac{n}", [P, G, F3]) for n in range(2)]
    oh = [s.sb(f"oh{n}", [P, P, G], BF16) for n in range(2)]
    ohT = [s.sb(f"ohT{n}", [P, G, P]) for n in range(2)]
    prod = s.sb("prod", [P, G, H, DK])
    pX = s.pb("pX")
    pU = [s.pb(f"pU{n}", [P, HG, F3]) for n in range(2)]
    pO = s.pb("pO", [P, G, P], BF16)
    pQ = [s.pb(f"pQ{n}", [P, G, DK]) for n in range(2)]
    (s_lg, s_lt, s_ltc, s_oh, s_ot, s_otc, s_q, s_att, s_link, s_m, s_init) = [
        s.sem(n) for n in ("lg", "lt", "ltc", "oh", "ot", "otc", "q", "att", "link", "m", "init")]
    s_u, s_tu, s_fr = [[s.sem(f"{n}{h}") for h in range(2)] for n in ("u", "tu", "fr")]
    s_sin = s.sem("sin")
    s_g = [s.sem(f"g{n}") for n in range(2)]
    s_v = [s.sem(f"v{n}") for n in range(2)]
    s_idx = s.sem("idx")
    s_turn = s.sem("turn")
    block = s.ctx.enter_context(nc.Block())
    word4 = rec[:].bitcast(I32)

    @block.gpsimd
    def _(pool):
        with pool.Fori(0, NI) as i:
            for h in range(2):
                pool.wait_ge(s_idx, 2 * i + h + 1)
                pool.wait_ge(s_att, 2 * i + h + 1)
                pool.wait_ge(s_v[h], 32 * i)
                pool.sem_inc(s_turn, 1)
                for t in range(G):
                    nc.gpsimd.indirect_dma_start(row[h][:, t, 0:2 * PROJ], None, table,
                                                 bass.IndirectOffsetOnAxis(idx[h][:, t:t + 1], 0)).then_inc(s_g[h], 16)

    @block.sync
    def _(sp):
        with sp.Fori(0, NI) as i:
            for h in range(2):
                t0 = i * 2 * G + h * G
                sp.wait_ge(s_g[h], 16 * G * (i + 1))
                sp.dma_start(spill[:, bass.ds(t0, G), 0:PROJ], row[h][:, :, 0:PROJ]).then_inc(s_v[h], 16)
                sp.wait_ge(s_sin, 2 * i + h + 1)
                sp.dma_start(spill[:, bass.ds(t0, G), PROJ:VW], row[h][:, :, 2 * PROJ:ROW]).then_inc(s_v[h], 16)
        for h in range(2):
            sp.wait_ge(s_v[h], 32 * NI)

    @block.scalar
    def _(act):
        act.wait_ge(s_att, 2)
        with act.Fori(0, NI) as i:
            for h in range(2):
                n = 2 * i + h
                t0 = n * G
                act.wait_ge(s_g[h], 16 * G * i)
                nc.scalar.activation(idx[h][:], word4[:, bass.ds(t0, G), 4], ACT.Copy).then_inc(s_idx, 1)
                act.wait_ge(s_lt, n)
                nc.scalar.activation(logs[h][:, 0:G * REC], rec[:, bass.ds(t0, G), :].rearrange("p t f -> p (t f)"), ACT.Copy).then_inc(s_lg, 1)
                act.wait_ge(s_lt, n + 1)
                nc.scalar.activation(logT[h][:], pX[0:G * REC, 0:P], ACT.Copy).then_inc(s_ltc, 1)
                for u in range(2):
                    act.wait_ge(s_u[u], n + 1)
                    act.wait_ge(s_fr[u], n)
                    nc.scalar.activation(turns[:, u], pU[u][:], ACT.Copy, bias=MAGIC).then_inc(s_tu[u], 1)
                act.wait_ge(s_ot, n + 1)
                act.wait_ge(s_q, n)
                nc.scalar.activation(ohT[h][:], pO[:], ACT.Copy).then_inc(s_otc, 1)
                act.wait_ge(s_fr[1], n + 1)
                act.wait_ge(s_v[h], 32 * i)
                act.wait_ge(s_att, n + 1)
                nc.scalar.activation(row[h][:, :, 2 * PROJ:ROW], frac[h][:, :, 0:2 * TD], ACT.Sin, scale=-2 * math.pi)
                nc.scalar.activation(eq[h][:], frac[h][:, :, 2 * TD:F3], ACT.Sin, scale=-2 * math.pi).then_inc(s_sin, 1)

    @block.tensor
    def _(pe):
        with pe.Fori(0, NI) as i:
            for h in range(2):
                n = 2 * i + h
                t0 = n * G
                _, tiles = nc.values_load_multi_w_load_instructions(
                    k.otile[d][0:1, bass.ds(t0, G)], engines=[nc.tensor.engine], min_val=0, max_val=S.NO - 1,
                    skip_runtime_bounds_check_because="an owner's tile")
                pe.wait_ge(s_lg, n + 1)
                pe.wait_ge(s_ltc, n)
                nc.tensor.transpose(pX[:, 0:P], logs[h][:], k.ident[:]).then_inc(s_lt, 1)
                pe.wait_ge(s_ltc, n + 1)
                for u in range(2):
                    pe.wait_ge(s_fr[u], n)
                    nc.tensor.matmul(pU[u][:].rearrange("p t f -> p (t f)"), logT[h][:], blk[:, u * HG * F3:(u + 1) * HG * F3],
                                     start=True, stop=True).then_inc(s_u[u], 1)
                pe.wait_ge(s_oh, n + 1)
                pe.wait_ge(s_otc, n)
                for t in range(G):
                    last = nc.tensor.transpose(pO[:, t, :], oh[h][:, :, t], k.ident_b[:])
                last.then_inc(s_ot, 1)
                pe.wait_ge(s_otc, n + 1)
                pe.wait_ge(s_att, n + 1)
                for t in range(G):
                    last = nc.tensor.matmul(pQ[h][:, t, :], ohT[h][:, t, :], k.qs[:, bass.ds(tiles[t] * DK, DK)], start=True, stop=True)
                last.then_inc(s_q, 1)

    @block.vector
    def _(dve):
        nc.vector.memset(logs[0][:], 0.0).then_inc(s_att, 1)
        nc.vector.memset(logs[1][:], 0.0).then_inc(s_att, 1)

        def features(n, h):
            dve.wait_ge(s_ot, n)
            nc.vector.tensor_tensor(oh[h][:], bc(k.lo[d][:, bass.ds(n * G, G)], 1, P), k.ramp16[:, :, 0:G], ALU.is_equal).then_inc(s_oh, 1)
            dve.wait_ge(s_sin, n)
            for u in range(2):
                dve.wait_ge(s_tu[u], n + 1)
                nc.vector.scalar_tensor_tensor(out=frac[h][:, u * HG:(u + 1) * HG, :], in0=turns[:, u], scalar=MAGIC, in1=pU[u][:],
                                               op0=ALU.subtract, op1=ALU.subtract).then_inc(s_fr[u], 1)

        def score(n, h, turn):
            link, _ = chain(dve, s_link, n * 2)
            dve.wait_ge(s_q, n + 1)
            dve.wait_ge(s_sin, n + 1)
            link(nc.vector.tensor_tensor(pQ[h][:, :, QC:DK], pQ[h][:, :, QC:DK], eq[h][:], ALU.add))
            dve.wait_ge(s_g[h], 16 * G * (turn + 1))
            link(nc.vector.tensor_tensor(prod[:], row[h][:, :, PROJ:PROJ + H * DK].rearrange("p t (h f) -> p t h f", h=H),
                                         bc(pQ[h][:], 2, H), ALU.mult))
            nc.vector.tensor_reduce(att[:, bass.ds(n * G, G), :], prod[:], op=ALU.add, axis=AX).then_inc(s_att, 1)

        features(0, 0)
        if NI > 1:
            with dve.Fori(0, NI - 1) as i:
                features(2 * i + 1, 1)
                score(2 * i, 0, i)
                features(2 * i + 2, 0)
                score(2 * i + 1, 1, i)
        features(2 * NI - 1, 1)
        score(2 * NI - 2, 0, NI - 1)
        score(2 * NI - 1, 1, NI - 1)


def softmax(nc, k, S, d, att_d, keys, alpha_d):
    TP, SPn, H, NT2 = S.TP, S.SP, S.H, S.NT2
    C = TP * P
    SCALE = 1.0 / math.sqrt(S.DK)
    with ExitStack() as ctx:
        s = Scope(nc, ctx, f"soft{d}")
        a = s.sb("a", [SPn, H, C])
        m = s.sb("m", [SPn, H, C])
        v = s.sb("v", [SPn, H, C])
        key = s.sb("key", [SPn, C + 2])
        run = s.sb("run", [SPn, C + 1])
        low = s.sb("low", [SPn, C])
        stop = s.sb("stop", [SPn, C])
        ends = s.sb("ends", [SPn, 3 + 1, H])
        keep = s.sb("keep", [H, 3, P])
        carry = s.sb("carry", [H, P + 2])
        cin = s.sb("cin", [SPn, H])
        zero = s.sb("zero", [P, P])
        pE = s.pb("pE")
        pF = s.pb("pF")
        s_in, s_a, s_dve, s_sub, s_exp, s_c, s_t, s_e, s_f, s_o, s_k, s_x = [
            s.sem(n) for n in ("in", "a", "dve", "sub", "exp", "c", "t", "e", "f", "o", "k", "x")]
        block = ctx.enter_context(nc.Block())
        w = NT2 - SPn * TP
        NIN = 1 + 2 * (SPn > 1)

        @block.sync
        def _(sp):
            kv = keys.rearrange("t e -> (t e)")
            sp.wait_ge(s_k, 1)
            sp.dma_start(key[:, 1:C + 1], kv[0:SPn * C].rearrange("(p c) -> p c", p=SPn)).then_inc(s_in, 16)
            if SPn > 1:
                with nc.allow_non_contiguous_dma(reason="one word of each partition"):
                    sp.dma_start(key[1:SPn, 0:1], kv[0:SPn * C].rearrange("(p c) -> p c", p=SPn)[0:SPn - 1, C - 1:C]).then_inc(s_in, 16)
                    sp.dma_start(key[0:SPn - 1, C + 1:C + 2], kv[0:SPn * C].rearrange("(p c) -> p c", p=SPn)[1:SPn, 0:1]).then_inc(s_in, 16)
            for h in range(H):
                sp.dma_start(a[:, h, :].rearrange("p (t e) -> p t e", e=P),
                             att_d[0:SPn * TP, h, :].rearrange("(p t) e -> p t e", p=SPn)).then_inc(s_a, 16)
            for h in range(H):
                sp.wait_ge(s_o, h + 1)
                sp.dma_start(alpha_d[0:SPn * TP, h, :].rearrange("(p t) e -> p t e", p=SPn),
                             a[:, h, :].rearrange("p (t e) -> p t e", e=P)).then_inc(s_x, 16)
            nz = 0
            rest = alpha_d[SPn * TP:NT2, :, :].rearrange("t h e -> (t h) e")
            while nz * P < w * H:
                r = min(P, w * H - nz * P)
                sp.dma_start(rest[nz * P:nz * P + r, :], zero[0:r, :]).then_inc(s_x, 16)
                nz += 1
            sp.wait_ge(s_x, 16 * (H + nz))

        @block.tensor
        def _(pe):
            for f in range(3):
                pe.wait_ge(s_c, f + 1)
                nc.tensor.transpose(pE[0:H, f * P:f * P + SPn], ends[:, f, :], k.ident[0:SPn, 0:SPn]).then_inc(s_t, 1)
            for n in range(4):
                pe.wait_ge(s_c, 4 + n)
                nc.tensor.transpose(pE[0:H, 0:SPn], ends[:, 3, :], k.ident[0:SPn, 0:SPn]).then_inc(s_t, 1)
                pe.wait_ge(s_e, n + 1)
                src = carry[:, 0:SPn] if n % 2 == 0 else carry[:, 2:SPn + 2]
                nc.tensor.transpose(pF[0:SPn, 0:H], src, k.ident[0:H, 0:H]).then_inc(s_f, 1)

        @block.scalar
        def _(act):
            for h in range(H):
                act.wait_ge(s_sub, h + 1)
                nc.scalar.activation(a[:, h, :], a[:, h, :], ACT.Exp, scale=SCALE).then_inc(s_exp, 1)

        @block.vector
        def _(dve):
            link, _ = chain(dve, s_dve)
            link(nc.vector.memset(zero[:], 0.0))
            link(nc.vector.memset(key[:, 0:1], -2.0))
            nc.vector.memset(key[:, C + 1:C + 2], -2.0).then_inc(s_k, 1)
            dve.wait_ge(s_in, 16 * NIN)
            link(nc.vector.tensor_tensor(run[:], key[:, 1:C + 2], key[:, 0:C + 1], ALU.is_equal))
            link(nc.vector.tensor_scalar(low[:], run[:, 0:C], -LOW, LOW, ALU.mult, ALU.add))
            link(nc.vector.tensor_scalar(stop[:], run[:, 1:C + 1], -1.0, 1.0, ALU.mult, ALU.add))
            for f, src in enumerate((low[:, 0:C], run[:, 0:C], run[:, 1:C + 1])):
                link(nc.vector.tensor_reduce(cin[:, f:f + 1], src, op=ALU.min, axis=AX))
                nc.vector.tensor_copy(ends[:, f, :], cin[:, f:f + 1].broadcast_to([SPn, H])).then_inc(s_c, 1)
                dve.wait_ge(s_t, f + 1)
                link(nc.vector.tensor_copy(keep[:, f, 0:SPn], pE[0:H, f * P:f * P + SPn]))
            dve.wait_ge(s_a, 16 * H)

            def scans(n, back, data0, src, dst, form, first, op0, op1):
                def at(x):
                    return x[:, ::-1] if back else x
                for h in range(H):
                    last = nc.vector.tensor_tensor_scan(at(dst[:, h, :]), at(data0), at(src[:, h, :]), first, op0, op1)
                link(last)
                link(nc.vector.memset(carry[:], first))
                edge = 0 if back else C - 1
                nc.vector.tensor_copy(ends[:, 3, :], dst[:, :, edge]).then_inc(s_c, 1)
                dve.wait_ge(s_t, 4 + n)
                nc.vector.tensor_tensor_scan(at(carry[:, 1:SPn + 1]), at(keep[:, form, 0:SPn]), at(pE[0:H, 0:SPn]), first, op0, op1).then_inc(s_e, 1)
                dve.wait_ge(s_f, n + 1)
                link(nc.vector.tensor_copy(cin[:], pF[0:SPn, 0:H]))
                for h in range(H):
                    last = nc.vector.tensor_tensor_scan(at(dst[:, h, :]), at(data0), at(src[:, h, :]), cin[:, h:h + 1], op0, op1)
                link(last)

            def last_of_run(n):
                for h in range(H):
                    last = nc.vector.tensor_tensor(m[:, h, :], m[:, h, :], stop[:], ALU.mult)
                link(last)
                scans(n, True, run[:, 1:C + 1], m, v, 2, 0.0, ALU.mult, ALU.add)

            scans(0, False, low[:], a, m, 0, LOW, ALU.add, ALU.max)
            last_of_run(1)
            for h in range(H):
                nc.vector.tensor_tensor(a[:, h, :], a[:, h, :], v[:, h, :], ALU.subtract).then_inc(s_sub, 1)
            dve.wait_ge(s_exp, H)
            scans(2, False, run[:, 0:C], a, m, 1, 0.0, ALU.mult, ALU.add)
            last_of_run(3)
            for h in range(H):
                link(nc.vector.tensor_scalar(v[:, h, :], v[:, h, :], 1e-16, None, ALU.add))
                link(nc.vector.reciprocal(v[:, h, :], v[:, h, :]))
                nc.vector.tensor_tensor(a[:, h, :], a[:, h, :], v[:, h, :], ALU.mult).then_inc(s_o, 1)


def aggregate(nc, k, S, d, spill, alpha_d):
    NT, G, DK, PROJ, TD, H, VW, NB, NT2, OUT = S.NT, S.G, S.DK, S.PROJ, S.TD, S.H, S.VW, S.NB, S.NT2, S.OUT
    NI = NT // (2 * G)
    with ExitStack() as ctx:
        s = Scope(nc, ctx, f"agg{d}")
        al = s.sb("al", [P, NT2, H])
        with ExitStack() as ctx2:
            s2 = Scope(nc, ctx2, f"al{d}")
            alT = s2.sb("alT", [P, NB, P])
            s_i, s_t, s_c, s_z = s2.sem("i"), s2.sem("t"), s2.sem("c"), s2.sem("z")
            pA = [s2.pb(f"pA{n}", [P, 4, P]) for n in range(2)]
            block = ctx2.enter_context(nc.Block())
            loads = [list(range(b, min(b + 4, NB))) for b in range(0, NB, 4)]

            @block.sync
            def _(sp):
                sp.dma_start(alT[:], alpha_d.rearrange("(b t) h e -> (t h) b e", t=32)).then_inc(s_i, 16)

            @block.tensor
            def _(pe):
                pe.wait_ge(s_i, 16)
                for n, bs in enumerate(loads):
                    if n >= 2:
                        pe.wait_ge(s_c, n - 1)
                    for j, b in enumerate(bs):
                        last = nc.tensor.transpose(pA[n % 2][:, j, :], alT[:, b, :], k.ident[:])
                    last.then_inc(s_t, 1)

            @block.scalar
            def _(act):
                for n, bs in enumerate(loads):
                    act.wait_ge(s_t, n + 1)
                    nc.scalar.activation(al[:, bs[0] * 32:(bs[-1] + 1) * 32, :].rearrange("p t h -> p (t h)"),
                                         pA[n % 2][:, 0:len(bs), :].rearrange("p b e -> p (b e)"), ACT.Copy).then_inc(s_c, 1)

            @block.vector
            def _(dve):
                if d == 0:
                    nc.vector.memset(k.acc[:], 0.0)

        with ExitStack() as ctx2:
            s2 = Scope(nc, ctx2, f"sum{d}")
            row = [s2.sb(f"row{n}", [P, G, VW]) for n in range(2)]
            oh = [s2.sb(f"oh{n}", [P, G, P]) for n in range(2)]
            mark = s2.sb("mark", [P, 1])
            pS = [s2.pb(f"pS{n}", [P, 2, VW]) for n in range(4)]
            s_v = [s2.sem(f"v{n}") for n in range(2)]
            s_w, s_p, s_add = s2.sem("w"), s2.sem("p"), s2.sem("add")
            block = ctx2.enter_context(nc.Block())

            @block.sync
            def _(sp):
                with sp.Fori(0, NI) as i:
                    for h in range(2):
                        sp.wait_ge(s_p, (2 * i + h) * (G // 2))
                        sp.dma_start(row[h][:], spill[:, bass.ds((2 * i + h) * G, G), :]).then_inc(s_v[h], 16)

            @block.tensor
            def _(pe):
                nc.tensor.matmul(pS[0][:, 0, :], k.ident[:], k.acc[:, 0, 0:VW], start=True, stop=True).then_inc(s_p, G // 2)
                with pe.Fori(0, NI) as i:
                    for h in range(2):
                        n = 2 * i + h
                        pe.wait_ge(s_w, n + 1)
                        for t in range(G):
                            if t % 2 == 0:
                                pe.wait_ge(s_add, n * G + t + 2)
                            last = nc.tensor.matmul(pS[t // 2 % 4][:, t % 2, :], oh[h][:, t, :], row[h][:, t, :], start=True, stop=True)
                            if t % 2:
                                last.then_inc(s_p, 1)

            @block.vector
            def _(dve):
                nc.vector.memset(mark[:], 0.0).then_inc(s_add, G)

                def weigh(n, h, turn):
                    dve.wait_ge(s_p, n * (G // 2))
                    nc.vector.tensor_tensor(oh[h][:], bc(k.lo[d][:, bass.ds(n * G, G)], 2, P), bc(k.ramp[:], 1, G), ALU.is_equal)
                    dve.wait_ge(s_v[h], 16 * (turn + 1))
                    r = row[h][:, :, 0:H * DK].rearrange("p t (h f) -> p t h f", h=H)
                    nc.vector.tensor_tensor(r, r, bc(al[:, bass.ds(n * G, G), :], 3, DK), ALU.mult).then_inc(s_w, 1)

                def add(n):
                    _, tiles = nc.values_load_multi_w_load_instructions(
                        k.otile[d][0:1, bass.ds(n * G, G)], engines=[nc.vector.engine], min_val=0, max_val=S.NO - 1,
                        skip_runtime_bounds_check_because="an owner's tile")
                    for t in range(G):
                        if t % 2 == 0:
                            dve.wait_ge(s_p, (n + 1) * (G // 2) + t // 2 + 1)
                        dve.wait_ge(s_add, (n + 1) * G + t - 1)
                        o = k.acc[:, t % 2, bass.ds(tiles[t] * VW, VW)]
                        nc.vector.tensor_tensor(o, o, pS[t // 2 % 4][:, t % 2, :], ALU.add).then_inc(s_add, 1)

                weigh(0, 0, 0)
                if NI > 1:
                    with dve.Fori(0, NI - 1) as i:
                        weigh(2 * i + 1, 1, i)
                        add(2 * i)
                        weigh(2 * i + 2, 0, i + 1)
                        add(2 * i + 1)
                weigh(2 * NI - 1, 1, NI - 1)
                add(2 * NI - 2)
                add(2 * NI - 1)


def output(nc, k, S, x, ntype, Wa, ba, gamma, beta, out):
    T, OUT, IN, KC = S.T, S.OUT, S.IN, S.KC
    OC = OUT // P
    full = S.NO - 1
    with ExitStack() as ctx:
        s = Scope(nc, ctx, "out")
        W = s.sb("W", [P, OC, T, IN])
        B = s.sb("B", [T, 3, IN])
        tid_i = s.sb("tid_i", [T, 1], I32)
        tid = s.sb("tid", [T, 1])
        xr = s.sb("xr", [P, IN])
        ty = s.sb("ty", [P, P], I32)
        aT = s.sb("aT", [P, OC, P])
        am = s.sb("am", [P, T, OC, P])
        W2 = am[:].rearrange("p t c n -> p t (c n)")[:, :, 0:IN]
        oneT = s.sb("oneT", [T, P])
        y = s.sb("y", [P, IN])
        z = s.sb("z", [P, IN])
        sq = s.sb("sq", [P, IN])
        st = s.sb("st", [P, 8])
        pT, pP, pG = s.pb("pT"), s.pb("pP"), s.pb("pG")
        s_w, s_w2, s_id, s_wr, s_x, s_aT, s_aTc, s_m, s_p, s_y, s_o, s_link, s_q, s_sq = [
            s.sem(n) for n in ("w", "w2", "id", "wr", "x", "aT", "aTc", "m", "p", "y", "o", "link", "q", "sq")]
        block = ctx.enter_context(nc.Block())

        @block.sync
        def _(sp):
            for c in range(OC):
                sp.dma_start(W[:, c], Wa[:, c * P:(c + 1) * P, :].rearrange("t p n -> p t n")).then_inc(s_w, 16)
            for j, b in enumerate((ba, gamma, beta)):
                sp.dma_start(B[:, j, :], b).then_inc(s_w, 16)
            for c in range(OC):
                sp.wait_ge(s_wr, c)
                sp.dma_start(W2, Wa[:, OUT + c * P:OUT + (c + 1) * P, :].rearrange("t p n -> p t n")).then_inc(s_w2, 16)

            def tile(rows, o):
                sp.wait_ge(s_y, o)
                sp.dma_start(xr[0:rows, :], x[bass.ds(o * P, rows), :]).then_inc(s_x, 16)
                sp.dma_start(ty[:, 0:rows], bc(ntype[bass.ds(o * P, rows)], 0, P)).then_inc(s_x, 16)
                sp.wait_ge(s_y, o + 1)
                sp.dma_start(out[bass.ds(o * P, rows), :], z[0:rows, :]).then_inc(s_o, 16)
            if full:
                with sp.Fori(0, full) as o:
                    tile(P, o)
            tile(S.LAST, full)
            sp.wait_ge(s_o, 16 * S.NO)

        @block.gpsimd
        def _(pool):
            nc.gpsimd.iota(tid_i[:], pattern=[[0, 1]], base=0, channel_multiplier=1).then_inc(s_id, 1)
            with pool.Fori(0, S.NO) as o:
                pool.wait_ge(s_aT, o)
                nc.gpsimd.tensor_tensor(k.cur_acc[:], k.acc[:, 0, bass.ds(o * OUT, OUT)], k.acc[:, 1, bass.ds(o * OUT, OUT)],
                                        ALU.add).then_inc(s_q, 1)

        @block.tensor
        def _(pe):
            def tile(rows, o):
                pe.wait_ge(s_aTc, o)
                pe.wait_ge(s_y, o)
                for c in range(OC):
                    last = nc.tensor.transpose(pT[:, c * P:(c + 1) * P], k.cur_acc[:, c * P:(c + 1) * P], k.ident[:])
                last.then_inc(s_aT, 1)
                for t in range(T):
                    pe.wait_ge(s_m, o * T + t + 1)
                    for c in range(OC):
                        nc.tensor.matmul(pP[0:rows, 0:IN], am[:, t, c, 0:rows], W[:, c, t, :], start=(t == 0 and c == 0), stop=False)
                nc.tensor.matmul(pP[0:rows, 0:IN], oneT[:, 0:rows], B[:, 0, :], start=False, stop=True)
                nc.tensor.matmul(pG[0:rows, 0:2 * IN], oneT[:, 0:rows], B[:, 1:3, :].rearrange("t a n -> t (a n)"),
                                 start=True, stop=True).then_inc(s_p, 1)

            def staged(rows, o):
                pe.wait_ge(s_q, o + 1)
                tile(rows, o)
            pe.wait_ge(s_wr, OC)
            if full:
                with pe.Fori(0, full) as o:
                    staged(P, o)
            staged(S.LAST, full)

        @block.scalar
        def _(act):
            def tile(rows, o):
                act.wait_ge(s_aT, o + 1)
                act.wait_ge(s_m, o * T)
                nc.scalar.activation(aT[:], pT[:, 0:OC * P].rearrange("p (c n) -> p c n", c=OC), ACT.Copy).then_inc(s_aTc, 1)
                for r in range(2):
                    act.wait_ge(s_sq, 4 * o + 2 * r + 1)
                    nc.scalar.activation(st[0:rows, 5:6], st[0:rows, 4:5], ACT.Sqrt).then_inc(s_sq, 1)
            if full:
                with act.Fori(0, full) as o:
                    tile(P, o)
            tile(S.LAST, full)

        @block.vector
        def _(dve):
            link, _ = chain(dve, s_link)
            dve.wait_ge(s_w, 16 * (OC + 3))
            dve.wait_ge(s_id, 1)
            link(nc.vector.tensor_copy(tid[:], tid_i[:]))
            for c in range(OC):
                dve.wait_ge(s_w2, 16 * (c + 1))
                nc.vector.tensor_tensor(W[:, c], W[:, c], W2, ALU.add).then_inc(s_wr, 1)
            PER = 19

            def tile(rows, o):
                link, n_link = chain(dve, s_link, 1 + o * PER)
                dve.wait_ge(s_x, 32 * (o + 1))
                link(nc.vector.tensor_scalar(oneT[:, 0:rows], ty[0:T, 0:rows], tid[:, 0:1], None, ALU.is_equal))
                dve.wait_ge(s_aTc, o + 1)
                for t in range(T):
                    nc.vector.scalar_tensor_tensor(out=am[:, t, :, 0:rows], in0=bc(ty[:, 0:rows], 1, OC), scalar=float(t),
                                                   in1=aT[:, :, 0:rows], op0=ALU.is_equal, op1=ALU.mult).then_inc(s_m, 1)
                dve.wait_ge(s_p, o + 1)
                R = slice(0, rows)
                link(nc.vector.tensor_tensor(y[R, :], xr[R, :], pP[R, 0:IN], ALU.add))

                def normalise(dst_, r):
                    link(nc.vector.tensor_reduce(st[R, 0:1], y[R, :], op=ALU.add, axis=AX))
                    link(nc.vector.tensor_scalar(st[R, 1:2], st[R, 0:1], 1.0 / IN, None, ALU.mult))
                    link(nc.vector.tensor_scalar(y[R, :], y[R, :], st[R, 1:2], None, ALU.subtract))
                    link(nc.vector.tensor_tensor(sq[R, :], y[R, :], y[R, :], ALU.mult))
                    link(nc.vector.tensor_reduce(st[R, 3:4], sq[R, :], op=ALU.add, axis=AX))
                    nc.vector.tensor_scalar(st[R, 4:5], st[R, 3:4], 1.0 / IN, LN_EPS, ALU.mult, ALU.add).then_inc(s_sq, 1)
                    dve.wait_ge(s_sq, 4 * o + 2 * r + 2)
                    link(nc.vector.reciprocal(st[R, 6:7], st[R, 5:6]))
                    return nc.vector.tensor_scalar(dst_[R, :], y[R, :], st[R, 6:7], None, ALU.mult)

                link(normalise(y, 0))
                link(nc.vector.tensor_tensor(y[R, :], y[R, :], pG[R, 0:IN], ALU.mult))
                link(nc.vector.tensor_tensor(y[R, :], y[R, :], pG[R, IN:2 * IN], ALU.add))
                link(nc.vector.tensor_tensor(y[R, :], y[R, :], xr[R, :], ALU.add))
                dve.wait_ge(s_o, 16 * o)
                link(normalise(z, 1))
                nc.vector.tensor_copy(st[R, 7:8], st[R, 6:7]).then_inc(s_y, 1)
                assert n_link[0] == PER, n_link
            if full:
                with dve.Fori(0, full) as o:
                    tile(P, o)
            tile(S.LAST, full)


class Kept:
    pass


def gnn_resnorm(nc, x, src, dst, edge_attr_5, node_type_19, Wk, bk, Wq, bq, Wv, bv, Wa, ba, gamma, beta, w_time, b_time, out):
    Scope.held = []
    S = Sizes(x, dst, Wk, Wa, w_time)
    recs = [nc.dram_tensor(f"recs{d}", [P * S.NT, S.REC], F32, kind="Internal").ap() for d in range(2)]
    table = nc.dram_tensor("table", [S.N, 2 * S.PROJ], F32, kind="Internal").ap()
    spill = [nc.dram_tensor(f"spill{d}", [P, S.NT, S.VW], F32, kind="Internal").ap() for d in range(2)]
    keys = [nc.dram_tensor(f"keys{d}", [S.NT2, P], F32, kind="Internal").ap() for d in range(2)]
    att = [nc.dram_tensor(f"att{d}", [S.NT2, S.H, P], F32, kind="Internal").ap() for d in range(2)]
    alpha = [nc.dram_tensor(f"alpha{d}", [S.NT2, S.H, P], F32, kind="Internal").ap() for d in range(2)]
    with ExitStack() as ctx:
        s = Scope(nc, ctx, "kept")
        k = Kept()
        k.ident = s.sb("ident", [P, P])
        k.ident_b = s.sb("ident_b", [P, P], BF16)
        k.ramp_i = s.sb("ramp_i", [P, P], I32)
        k.ramp = s.sb("ramp", [P, P])
        k.ramp16 = s.sb("ramp16", [P, P, S.SG], BF16)
        k.qs = s.sb("qs", [P, S.NO * S.DK])
        k.otile = [s.sb(f"otile{d}", [1, S.NT], I32) for d in range(2)]
        k.lo = [s.sb(f"lo{d}", [P, S.NT], BF16) for d in range(2)]
        constants(nc, k, S)
        project(nc, k, S, x, node_type_19, Wk, bk, Wq, bq, Wv, bv, table)
        sort_edges(nc, k, S, src, dst, edge_attr_5, recs)
        Scope.retire(nc)
        for d in range(2):
            gather(nc, k, S, d, recs[d], table, spill[d], keys[d], att[d], w_time, b_time)
            softmax(nc, k, S, d, att[d], keys[d], alpha[d])
            Scope.retire(nc)
        k.acc = s.sb("acc", [P, 2, S.NO * S.OUT])
        k.cur_acc = s.sb("cur_acc", [P, S.OUT])
        for d in range(2):
            aggregate(nc, k, S, d, spill[d], alpha[d])
            Scope.retire(nc)
        output(nc, k, S, x, node_type_19, Wa, ba, gamma, beta, out)
        Scope.retire(nc)


_INS = ["x", "src", "dst", "edge_attr_5", "node_type_19", "L0_gnn_Wk", "L0_gnn_bk", "L0_gnn_Wq", "L0_gnn_bq", "L0_gnn_Wv",
        "L0_gnn_bv", "L0_gnn_Wa", "L0_gnn_ba", "L0_gnn_gamma", "L0_gnn_beta", "L0_gnn_w_time", "L0_gnn_b_time"]


def kernel(**inputs):
    import concourse.bacc as bacc
    from concourse.bass_utils import run_bass_kernel_spmd

    nc = bacc.Bacc("TRN2", target_bir_lowering=False, num_devices=1)
    arrays, args = {}, []
    for name in _INS:
        a = np.ascontiguousarray(inputs[name])
        arrays[f"in_{name}"] = a
        args.append(nc.dram_tensor(f"in_{name}", a.shape, mybir.dt.from_np(a.dtype), kind="ExternalInput").ap())
    out = nc.dram_tensor("out_x", inputs["x"].shape, F32, kind="ExternalOutput").ap()
    gnn_resnorm(nc, *args, out)
    r = run_bass_kernel_spmd(nc, [arrays], core_ids=[0])
    return r.results[0]["out_x"]
```

```python
import math
from contextlib import ExitStack

import numpy as np

import concourse.bass as bass
from concourse import mybir

F32 = mybir.dt.float32
BF16 = mybir.dt.bfloat16
I32 = mybir.dt.int32
ALU = mybir.AluOpType
ACT = mybir.ActivationFunctionType
AX = mybir.AxisListType.X

P = 128
MAGIC = 12582912.0
LOW = -1.0e38
PAD_LO = 128.0
LN_EPS = 1e-05


class Sizes:

    def __init__(self, x, dst, Wk, Wa, w_time):
        self.N, self.IN = x.shape
        self.E = dst.shape[0]
        self.T, _, self.PROJ = Wk.shape
        self.TD = w_time.shape[0]
        self.OUT = Wa.shape[1] // 2
        self.H = 4
        self.B = 4
        self.DK = (self.PROJ + self.TD) // self.H
        self.KC = self.IN // P
        self.NO = -(-self.N // P)
        self.LAST = self.N - (self.NO - 1) * P
        used = (self.N + self.T * (P - 1)) // P
        self.NBT = -(-used // (2 * self.B)) * 2
        self.NTT = self.NBT * self.B
        self.CN = self.N // P
        self.CE = self.E // P
        self.REST = self.E - self.CE * P
        self.SG = 16
        self.CT = -(-(self.CE + (self.REST > 0)) // (2 * self.SG)) * 2 * self.SG
        used = (self.E + self.NO * (2 * P - 1)) // (2 * P) * 2
        self.G = 8
        self.NT = -(-used // (2 * self.G)) * 2 * self.G
        self.TP = -(-used // P)
        self.SP = -(-used // self.TP)
        self.NB = -(-max(self.NT, self.SP * self.TP) // 32)
        self.NT2 = self.NB * 32
        self.REC = 5
        self.VW = self.PROJ + 2 * self.TD
        self.ROW = 2 * self.PROJ + 2 * self.TD


def chain(eng, sem, base=0):
    n = [0]

    def link(ins):
        n[0] += 1
        ins.then_inc(sem, 1)
        eng.wait_ge(sem, base + n[0])

    return link, n


def bc(ap, axis, count):
    shape = list(ap.shape)
    shape.insert(axis, count)
    return ap.unsqueeze(axis).broadcast_to(shape)


class Scope:

    held = []

    def __init__(self, nc, ctx, tag):
        self.nc, self.ctx, self.tag = nc, ctx, tag

    def sb(self, name, shape, dt=F32):
        return self.ctx.enter_context(self.nc.sbuf_tensor(f"{self.tag}_{name}", shape, dt))

    def pb(self, name, shape=(P, 512), dt=F32):
        return self.ctx.enter_context(self.nc.psum_tensor(f"{self.tag}_{name}", list(shape), dt))

    def sem(self, name):
        self.held.append(self.nc.alloc_semaphore(f"{self.tag}_{name}"))
        return self.held[-1]

    @classmethod
    def retire(cls, nc):
        nc.clear_and_free_semaphores(cls.held)
        cls.held = []
        nc.all_engine_barrier()


def constants(nc, k, S):
    with ExitStack() as ctx:
        s = Scope(nc, ctx, "const")
        s_pool = s.sem("pool")
        s_dve = s.sem("dve")
        block = ctx.enter_context(nc.Block())

        @block.gpsimd
        def _(pool):
            link, _ = chain(pool, s_pool)
            link(nc.gpsimd.memset(k.ident[:], 0.0))
            link(nc.gpsimd.affine_select(out=k.ident[:], in_=k.ident[:], compare_op=ALU.not_equal, fill=1.0,
                                         base=0, pattern=[[-1, P]], channel_multiplier=1))
            link(nc.gpsimd.iota(k.ramp_i[:], pattern=[[1, P]], base=0, channel_multiplier=0))
            link(nc.gpsimd.memset(k.ones[:], 1.0))
            link(nc.gpsimd.affine_select(out=k.below[:], in_=k.ones[:], compare_op=ALU.is_gt, fill=0.0,
                                         base=0, pattern=[[1, P]], channel_multiplier=-1))

        @block.vector
        def _(dve):
            link, _ = chain(dve, s_dve)
            dve.wait_ge(s_pool, 3)
            link(nc.vector.tensor_copy(k.ident_b[:], k.ident[:]))
            link(nc.vector.tensor_copy(k.ramp[:], k.ramp_i[:]))
            link(nc.vector.tensor_copy(k.ramp16[:], bc(k.ramp[:], 2, 16)))


def group_nodes(nc, k, S, ntype, slots):
    T, NO, CN, NTT, N = S.T, S.NO, S.CN, S.NTT, S.N
    RN = N - CN * P
    per = 512 // NO
    parts = [(t, min(t + per, T)) for t in range(0, T, per)]
    with ExitStack() as ctx:
        s = Scope(nc, ctx, "group")
        ty = s.sb("ty", [P, NO], I32)
        ids = s.sb("ids", [P, NO], I32)
        none = s.sb("none", [P, NTT], I32)
        one = s.sb("one", [P, T, NO])
        col = s.sb("col", [P, T, NO])
        place = s.sb("place", [P, T, NO])
        zero = s.sb("zero", [P, T * NO])
        st = s.sb("st", [P, 6, T])
        sti = s.sb("sti", [P, T], I32)
        ge = s.sb("ge", [1, T, NTT])
        tt = s.sb("tt", [1, NTT])
        slot = s.sb("slot", [P, NO])
        inval = s.sb("inval", [P, NO])
        slot_i = s.sb("slot_i", [P, 2, NO], I32)
        addr = s.sb("addr", [P, NO], I32)
        pB = [s.pb(f"pB{n}") for n in range(len(parts))]
        pC = [s.pb(f"pC{n}") for n in range(len(parts))]
        s_ids, s_ty, s_none, s_in, s_n, s_dve, s_one, s_sum, s_addr, s_scat, s_out = [
            s.sem(n) for n in ("ids", "ty", "none", "in", "n", "dve", "one", "sum", "addr", "scat", "out")]
        block = ctx.enter_context(nc.Block())
        NIN = 16 * ((CN > 0) + (RN > 0))

        @block.sync
        def _(sp):
            sp.wait_ge(s_ty, 1)
            if CN:
                sp.dma_start(ty[:, 0:CN], ntype[0:CN * P].rearrange("(p c) -> p c", p=P)).then_inc(s_in, 16)
            if RN:
                sp.dma_start(ty[0:RN, CN:CN + 1], ntype[CN * P:N].unsqueeze(1)).then_inc(s_in, 16)
            sp.wait_ge(s_none, 1)
            sp.dma_start(slots.rearrange("(p c) o -> p (c o)", p=P), none[:]).then_inc(s_n, 16)
            sp.wait_ge(s_scat, 16 * NO)
            sp.dma_start(k.nodes[:], slots.rearrange("(p c) o -> p (c o)", p=P)).then_inc(s_out, 16)
            sp.wait_ge(s_out, 16)

        @block.gpsimd
        def _(pool):
            if CN:
                nc.gpsimd.iota(ids[:, 0:CN], pattern=[[1, CN]], base=0, channel_multiplier=CN).then_inc(s_ids, 1)
            if RN:
                nc.gpsimd.iota(ids[:, CN:NO], pattern=[[0, 1]], base=CN * P, channel_multiplier=1).then_inc(s_ids, 1)
            pool.wait_ge(s_n, 16)
            pool.wait_ge(s_addr, 1)
            pool.wait_ge(s_ids, (CN > 0) + (RN > 0))
            for c in range(NO):
                nc.gpsimd.indirect_dma_start(slots, bass.IndirectOffsetOnAxis(addr[:, c:c + 1], 0), ids[:, c:c + 1], None,
                                             bounds_check=P * NTT - 1, oob_is_err=False).then_inc(s_scat, 16)
            pool.wait_ge(s_scat, 16 * NO)

        @block.tensor
        def _(pe):
            pe.wait_ge(s_one, 1)
            for n, (a, b) in enumerate(parts):
                w = (b - a) * NO
                x = one[:, a:b, :].rearrange("p t c -> p (t c)")
                nc.tensor.matmul(pB[n][:, 0:w], k.below[:], x, start=True, stop=True)
                last = nc.tensor.matmul(pC[n][:, 0:w], k.ones[:], x, start=True, stop=True)
            last.then_inc(s_sum, 1)

        @block.vector
        def _(dve):
            link, _ = chain(dve, s_dve)
            nc.vector.memset(ty[:], T).then_inc(s_ty, 1)
            nc.vector.memset(none[:], N).then_inc(s_none, 1)
            link(nc.vector.memset(zero[:], 0.0))
            dve.wait_ge(s_in, NIN)
            link(nc.vector.tensor_scalar(inval[:], ty[:], float(T), float(1 << 20), ALU.is_ge, ALU.mult))
            nc.vector.tensor_tensor(one[:], bc(ty[:], 1, T), bc(k.ramp[:, 0:T], 2, NO), ALU.is_equal).then_inc(s_one, 1)
            dve.wait_ge(s_sum, 1)
            for n, (a, b) in enumerate(parts):
                last = nc.vector.tensor_copy(col[:, a:b, :], pC[n][:, 0:(b - a) * NO].rearrange("p (t c) -> p t c", c=NO))
            link(last)
            flat = "p t c -> p (t c)"
            link(nc.vector.tensor_tensor_scan(place[:].rearrange(flat), col[:].rearrange(flat), zero[:], 0.0, ALU.add, ALU.add))
            link(nc.vector.tensor_copy(st[:, 0, :], place[:, :, NO - 1]))
            link(nc.vector.tensor_tensor(place[:], place[:], col[:], ALU.subtract))
            link(nc.vector.tensor_tensor(st[:, 1, :], st[:, 0, :], place[:, :, 0], ALU.subtract))
            link(nc.vector.tensor_scalar(sti[:], st[:, 1, :], float(P - 1), None, ALU.add))
            link(nc.vector.tensor_scalar(sti[:], sti[:], 7, None, ALU.logical_shift_right))
            link(nc.vector.tensor_copy(st[:, 2, :], sti[:]))
            link(nc.vector.tensor_tensor_scan(st[:, 3, :], st[:, 2, :], zero[:, 0:T], 0.0, ALU.add, ALU.add))
            link(nc.vector.tensor_tensor(st[:, 4, :], st[:, 3, :], st[:, 2, :], ALU.subtract))
            link(nc.vector.scalar_tensor_tensor(out=st[:, 5, :], in0=st[:, 4, :], scalar=float(P), in1=place[:, :, 0],
                                                op0=ALU.mult, op1=ALU.subtract))
            for n, (a, b) in enumerate(parts):
                last = nc.vector.tensor_tensor(place[:, a:b, :], place[:, a:b, :],
                                               pB[n][:, 0:(b - a) * NO].rearrange("p (t c) -> p t c", c=NO), ALU.add)
            link(last)
            link(nc.vector.tensor_tensor(place[:], place[:], bc(st[:, 5, :], 2, NO), ALU.add))
            link(nc.vector.tensor_tensor(place[:], place[:], one[:], ALU.mult))
            link(nc.vector.tensor_reduce(slot[:], place[:].rearrange("p t c -> p c t"), op=ALU.add, axis=AX))
            link(nc.vector.tensor_copy(slot_i[:, 0, :], slot[:]))
            link(nc.vector.tensor_scalar(slot_i[:, 1, :], slot_i[:, 0, :], P - 1, None, ALU.bitwise_and))
            link(nc.vector.tensor_scalar(slot_i[:, 0, :], slot_i[:, 0, :], 7, None, ALU.logical_shift_right))
            link(nc.vector.scalar_tensor_tensor(out=slot[:], in0=slot_i[:, 1, :], scalar=float(NTT), in1=slot_i[:, 0, :],
                                                op0=ALU.mult, op1=ALU.add))
            nc.vector.tensor_tensor(addr[:], slot[:], inval[:], ALU.add).then_inc(s_addr, 1)
            link(nc.vector.tensor_tensor(ge[:], bc(k.ramp[0:1, 0:NTT], 1, T), bc(st[0:1, 4, :], 2, NTT), ALU.is_ge))
            link(nc.vector.tensor_reduce(tt[:], ge[:].rearrange("p t c -> p c t"), op=ALU.add, axis=AX))
            link(nc.vector.tensor_scalar(k.ttype[:], tt[:], -1.0, None, ALU.add))


def tile_types(nc, k, S, eng, n):
    _, types = nc.values_load_multi_w_load_instructions(
        k.ttype[0:1, bass.ds(n * S.B, S.B)], engines=[eng.engine], min_val=0, max_val=S.T - 1,
        skip_runtime_bounds_check_because="a tile's type")
    return types


def in_turns(eng, count, body):
    if count > 2:
        with eng.Fori(0, count // 2 - 1) as i:
            body(2 * i, 0, i, True)
            body(2 * i + 1, 1, i, True)
    body(count - 2, 0, count // 2 - 1, True)
    body(count - 1, 1, count // 2 - 1, False)


def project(nc, k, S, x, Wk, bk, Wq, bq, Wv, bv, table, qtable):
    H, DK, PROJ, T, KC, B, NBT, N, IN = S.H, S.DK, S.PROJ, S.T, S.KC, S.B, S.NBT, S.N, S.IN
    TAIL = PROJ - (H - 1) * DK
    WN = 2 * PROJ + DK
    with ExitStack() as ctx:
        s = Scope(nc, ctx, "proj")
        W = s.sb("W", [P, KC, T, WN])
        Wqr = s.sb("Wqr", [P, KC, T, PROJ])
        bias = s.sb("bias", [1, T, WN])
        bqr = s.sb("bqr", [1, T, PROJ])
        idx = [s.sb(f"idx{h}", [P, B], I32) for h in range(2)]
        xr = [s.sb(f"xr{h}", [P, B, IN]) for h in range(2)]
        xT = s.sb("xT", [P, B, IN])
        kv = [s.sb(f"kv{h}", [P, B, WN]) for h in range(2)]
        pT = [s.pb(f"pT{n}", [P, 2, IN]) for n in range(2)]
        pP = [s.pb(f"pP{n}") for n in range(B)]
        s_w, s_wq, s_clr, s_idx, s_xT, s_xTc, s_p, s_kv, s_q, s_turn, s_dve = [
            s.sem(n) for n in ("w", "wq", "clr", "idx", "xT", "xTc", "p", "kv", "q", "turn", "dve")]
        s_g = [s.sem(f"g{h}") for h in range(2)]
        s_sc = [s.sem(f"sc{h}") for h in range(2)]
        block = ctx.enter_context(nc.Block())

        @block.sync
        def _(sp):
            for c in range(KC):
                r = slice(c * P, (c + 1) * P)
                sp.dma_start(Wqr[:, c, :, :], Wq[:, r, :].rearrange("t p n -> p t n")).then_inc(s_w, 16)
                sp.dma_start(W[:, c, :, 0:PROJ], Wv[:, r, :].rearrange("t p n -> p t n")).then_inc(s_w, 16)
                sp.dma_start(W[:, c, :, PROJ:2 * PROJ], Wk[:, r, :].rearrange("t p n -> p t n")).then_inc(s_w, 16)
            sp.dma_start(bias[:, :, 0:PROJ], bv.unsqueeze(0)).then_inc(s_w, 16)
            sp.dma_start(bias[:, :, PROJ:2 * PROJ], bk.unsqueeze(0)).then_inc(s_w, 16)
            sp.dma_start(bqr[:], bq.unsqueeze(0)).then_inc(s_w, 16)
            for h in range(2):
                sp.wait_ge(s_sc[h], 32 * B * (NBT // 2))
            if S.NO > 1:
                sp.dma_start(k.qs[:, 0:(S.NO - 1) * DK].rearrange("p (o f) -> p o f", f=DK),
                             qtable[0:(S.NO - 1) * P, :].rearrange("(o p) f -> p o f", p=P)).then_inc(s_q, 16)
            sp.dma_start(k.qs[0:S.LAST, (S.NO - 1) * DK:S.NO * DK], qtable[(S.NO - 1) * P:N, :]).then_inc(s_q, 16)
            sp.wait_ge(s_q, 32 if S.NO > 1 else 16)

        @block.gpsimd
        def _(pool):
            def gather_x(n, h):
                pool.wait_ge(s_idx, n + 1)
                pool.sem_inc(s_turn, 1)
                for j in range(B):
                    nc.gpsimd.indirect_dma_start(xr[h][:, j, :], None, x, bass.IndirectOffsetOnAxis(idx[h][:, j:j + 1], 0),
                                                 bounds_check=N - 1, oob_is_err=False).then_inc(s_g[h], 16)

            def body(n, h, turn, more):
                if more:
                    gather_x(n + 1, 1 - h)
                pool.wait_ge(s_kv, n + 1)
                pool.sem_inc(s_turn, 1)
                for j in range(B):
                    for t, a, b in ((table, 0, 2 * PROJ), (qtable, 2 * PROJ, WN)):
                        nc.gpsimd.indirect_dma_start(t, bass.IndirectOffsetOnAxis(idx[h][:, j:j + 1], 0), kv[h][:, j, a:b], None,
                                                     bounds_check=N - 1, oob_is_err=False).then_inc(s_sc[h], 16)
            nc.gpsimd.memset(xr[1][:], 0.0)
            nc.gpsimd.memset(xr[0][:], 0.0).then_inc(s_clr, 1)
            pool.wait_ge(s_clr, 1)
            gather_x(0, 0)
            in_turns(pool, NBT, body)

        @block.vector
        def _(dve):
            link, _ = chain(dve, s_dve)
            dve.wait_ge(s_w, 16 * (3 * KC + 3))
            for to, of in ((W, Wqr), (bias, bqr)):
                lead = [slice(None)] * (len(of.shape) - 1)

                def q(a, b):
                    return of[tuple(lead + [slice(a, b)])]

                def o(a, b):
                    return to[tuple(lead + [slice(2 * PROJ + a, 2 * PROJ + b)])]

                link(nc.vector.tensor_tensor(o(0, DK), q(0, DK), q(DK, 2 * DK), ALU.add))
                link(nc.vector.tensor_tensor(o(0, DK), o(0, DK), q(2 * DK, 3 * DK), ALU.add))
                link(nc.vector.tensor_tensor(o(0, TAIL), o(0, TAIL), q(3 * DK, PROJ), ALU.add))
            nc.vector.memset(k.qs[:, (S.NO - 1) * DK:S.NO * DK], 0.0).then_inc(s_wq, 1)

        @block.tensor
        def _(pe):
            pe.wait_ge(s_wq, 1)

            def body(n, h, turn, more):
                types = tile_types(nc, k, S, nc.tensor, n)
                pe.wait_ge(s_g[h], 16 * B * (turn + 1))
                pe.wait_ge(s_xTc, 2 * n)
                for j in range(B):
                    for c in range(KC):
                        last = nc.tensor.transpose(pT[j // 2][:, j % 2, c * P:(c + 1) * P], xr[h][:, j, c * P:(c + 1) * P], k.ident[:])
                    if j % 2:
                        last.then_inc(s_xT, 1)
                pe.wait_ge(s_kv, n)
                for j in range(B):
                    if j % 2 == 0:
                        pe.wait_ge(s_xTc, 2 * n + j // 2 + 1)
                    for c in range(KC):
                        nc.tensor.matmul(pP[j][:, 0:WN], xT[:, j, c * P:(c + 1) * P],
                                         W[:].rearrange("p c t n -> p c (t n)")[:, c, bass.ds(types[j] * WN, WN)],
                                         start=(c == 0), stop=False)
                    nc.tensor.matmul(pP[j][:, 0:WN], k.ones[0:1, :], bias[:].rearrange("p t n -> p (t n)")[:, bass.ds(types[j] * WN, WN)],
                                     start=False, stop=True).then_inc(s_p, 1)
            in_turns(pe, NBT, body)

        @block.scalar
        def _(act):
            def stage(n, h, turn):
                act.wait_ge(s_sc[h], 32 * B * turn)
                nc.scalar.activation(idx[h][:], k.nodes[:, bass.ds(n * B, B)], ACT.Copy).then_inc(s_idx, 1)

            def body(n, h, turn, more):
                if more:
                    stage(n + 1, 1 - h, turn + h)
                for j in range(2):
                    act.wait_ge(s_xT, 2 * n + j + 1)
                    act.wait_ge(s_p, n * B)
                    nc.scalar.activation(xT[:, 2 * j:2 * j + 2, :], pT[j][:], ACT.Copy).then_inc(s_xTc, 1)
                act.wait_ge(s_sc[h], 32 * B * turn)
                for j in range(B):
                    act.wait_ge(s_p, n * B + j + 1)
                    last = nc.scalar.activation(kv[h][:, j, :], pP[j][:, 0:WN], ACT.Copy)
                last.then_inc(s_kv, 1)
            stage(0, 0, 0)
            in_turns(act, NBT, body)


def one_hots(nc, S, k, oh_lo, oh_hi, piece, ramp_hi, par, col):
    for d in range(2):
        nc.vector.tensor_tensor(oh_lo[:, par, d], bc(piece[:, d, 0, bass.ds(col, S.SG)], 1, P), k.ramp16[:], ALU.is_equal)
        last = nc.vector.tensor_tensor(oh_hi[:, par, d], bc(piece[:, d, 1, bass.ds(col, S.SG)], 1, S.NO), ramp_hi[:], ALU.is_equal)
    return last


def sort_edges(nc, k, S, src, dst, edge_attr, recs):
    CT, CE, REST, SG, NO, NT, REC = S.CT, S.CE, S.REST, S.SG, S.NO, S.NT, S.REC
    NG = CT // SG
    with ExitStack() as ctx:
        s = Scope(nc, ctx, "sort")
        raw = s.sb("raw", [P, 2, CT], I32)
        own = s.sb("own", [P, 2, CT])
        piece = s.sb("piece", [P, 2, 2, CT], BF16)
        ea = s.sb("ea", [P, CT, 5])
        inval = s.sb("inval", [P, CT])
        ramp_hi = s.sb("ramp_hi", [P, NO, SG], BF16)
        oh_lo = s.sb("oh_lo", [P, 2, 2, P, SG], BF16)
        oh_hi = s.sb("oh_hi", [P, 2, 2, NO, SG], BF16)
        tri = s.sb("tri", [P, P])
        sel = s.sb("sel", [64, 32, P], BF16)
        base = s.sb("base", [P, 2, NO])
        count_owners(nc, k, S, src, dst, edge_attr, recs, raw, own, piece, ea, inval, ramp_hi, oh_lo, oh_hi, tri, sel, base)
        place_edges(nc, k, S, recs, raw, own, piece, ea, inval, ramp_hi, oh_lo, oh_hi, tri, sel, base)


def count_owners(nc, k, S, src, dst, edge_attr, recs, raw, own, piece, ea, inval, ramp_hi, oh_lo, oh_hi, tri, sel, base):
    CT, CE, REST, SG, NO, NT, REC = S.CT, S.CE, S.REST, S.SG, S.NO, S.NT, S.REC
    NG = CT // SG
    TC = -(-NT // 4)
    assert TC <= 512
    with ExitStack() as ctx:
        s = Scope(nc, ctx, "count")
        tmp = s.sb("tmp", [P, 2, CT], I32)
        padrec = s.sb("padrec", [P, NT // 8, REC])
        zero = s.sb("zero", [P, P])
        hs = s.sb("hs", [P, 2, NO])
        st = s.sb("st", [P, 4, NO])
        sti = s.sb("sti", [P, NO], I32)
        stc = s.sb("stc", [P, 2])
        ramp_ti = s.sb("ramp_ti", [NO, NT], I32)
        ge = s.sb("ge", [NO, NT])
        junk = s.sb("junk", [P, NO])
        pH = [s.pb(f"pH{d}") for d in range(2)]
        pO = [s.pb(f"pO{n}") for n in range(4)]
        s_in, s_ea, s_dve, s_c, s_oh, s_h, s_hc, s_o, s_oc, s_ot, s_pad, s_prep = [
            s.sem(n) for n in ("in", "ea", "dve", "c", "oh", "h", "hc", "o", "oc", "ot", "pad", "prep")]
        block = ctx.enter_context(nc.Block())

        @block.sync
        def _(sp):
            sp.wait_ge(s_c, 1)
            for d, a in enumerate((dst, src)):
                sp.dma_start(raw[:, d, 0:CE], a[0:CE * P].rearrange("(p c) -> p c", p=P)).then_inc(s_in, 16)
                if REST:
                    sp.dma_start(raw[0:REST, d, CE:CE + 1], a[CE * P:].unsqueeze(1)).then_inc(s_in, 16)
            sp.wait_ge(s_c, 2)
            sp.dma_start(ea[:, 0:CE, :], edge_attr[0:CE * P, :].rearrange("(p c) f -> p c f", p=P)).then_inc(s_ea, 16)
            if REST:
                sp.dma_start(ea[0:REST, CE, :], edge_attr[CE * P:, :]).then_inc(s_ea, 16)
            sp.wait_ge(s_c, 3)
            for d in range(2):
                r = recs[d].rearrange("(p c) f -> p c f", p=P)
                for n in range(8):
                    w = NT // 8
                    sp.dma_start(r[:, n * w:(n + 1) * w, :], padrec[:]).then_inc(s_pad, 16)
            sp.wait_ge(s_pad, 256)
            sp.wait_ge(s_ea, 32 if REST else 16)

        @block.gpsimd
        def _(pool):
            link, _ = chain(pool, s_prep)
            link(nc.gpsimd.iota(ramp_ti[:], pattern=[[1, NT]], base=0, channel_multiplier=0))
            link(nc.gpsimd.affine_select(out=tri[:], in_=k.ones[:], compare_op=ALU.is_gt, fill=0.0,
                                         base=0, pattern=[[-1, P]], channel_multiplier=1))
            link(nc.gpsimd.memset(sel[:], 0.0))
            v = sel[:].rearrange("r (d k) m -> r d k m", d=2)
            for off in (0, 16):
                for d in range(2):
                    link(nc.gpsimd.affine_select(out=v[:, d], in_=v[:, d], compare_op=ALU.not_equal, fill=1.0,
                                                 base=-off - 32 * d, pattern=[[-1, 16], [0, P]], channel_multiplier=1))

        @block.vector
        def _(dve):
            link, _ = chain(dve, s_dve)
            nc.vector.memset(raw[:, :, CE:CT], 100 * P).then_inc(s_c, 1)
            nc.vector.memset(ea[:, CE:CT, :], 0.0).then_inc(s_c, 1)
            link(nc.vector.memset(padrec[:], 0.0))
            nc.vector.memset(padrec[:, :, 3:4], -1.0).then_inc(s_c, 1)
            nc.vector.memset(zero[:], 0.0).then_inc(s_c, 1)
            link(nc.vector.tensor_scalar(st[:, 0, :], k.ramp[:, 0:NO], float(P), None, ALU.mult))
            link(nc.vector.tensor_copy(ramp_hi[:], bc(st[:, 0, :], 2, SG)))
            dve.wait_ge(s_in, 64 if REST else 32)
            link(nc.vector.tensor_copy(own[:], raw[:]))
            link(nc.vector.tensor_scalar(tmp[:], raw[:], P - 1, None, ALU.bitwise_and))
            link(nc.vector.tensor_copy(piece[:, :, 0, :], tmp[:]))
            link(nc.vector.tensor_tensor(piece[:, :, 1, :], own[:], tmp[:], ALU.subtract))
            link(nc.vector.tensor_scalar(inval[:], own[:, 0, :], 100.0 * P, float(1 << 20), ALU.is_ge, ALU.mult))
            with dve.Fori(0, NG // 2) as i:
                for par in range(2):
                    dve.wait_ge(s_h, 2 * i + par)
                    one_hots(nc, S, k, oh_lo, oh_hi, piece, ramp_hi, par, (2 * i + par) * SG).then_inc(s_oh, 1)
            dve.wait_ge(s_h, NG + 1)
            nc.vector.tensor_copy(hs[:, 0, :], pH[0][:, 0:NO])
            link(nc.vector.tensor_copy(hs[:, 1, :], pH[1][:, 0:NO]))
            nc.vector.tensor_copy(junk[:], pH[1][:, 0:NO]).then_inc(s_hc, 1)
            for d in range(2):
                dve.wait_ge(s_o, d + 1)
                link(nc.vector.tensor_scalar(sti[:], pO[1][:, 0:NO], float(2 * P - 1), None, ALU.add))
                link(nc.vector.tensor_scalar(sti[:], sti[:], 8, None, ALU.logical_shift_right))
                link(nc.vector.tensor_scalar(st[:, 1, :], sti[:], 2.0, None, ALU.mult))
                link(nc.vector.tensor_tensor_scan(st[:, 2, :], st[:, 1, :], zero[:, 0:NO], 0.0, ALU.add, ALU.add))
                link(nc.vector.tensor_tensor(st[:, 3, :], st[:, 2, :], st[:, 1, :], ALU.subtract))
                link(nc.vector.scalar_tensor_tensor(out=base[:, d, :], in0=st[:, 3, :], scalar=float(P), in1=pO[0][:, 0:NO],
                                                    op0=ALU.mult, op1=ALU.add))
                link(nc.vector.tensor_tensor(junk[:], st[:, 3, :], k.ident[:, 0:NO], ALU.mult))
                link(nc.vector.tensor_reduce(stc[:, d:d + 1], junk[:], op=ALU.add, axis=AX))
                dve.wait_ge(s_prep, 1)
                nc.vector.tensor_scalar(ge[:], ramp_ti[:], stc[0:NO, d:d + 1], None, ALU.is_ge).then_inc(s_oc, 1)
                dve.wait_ge(s_ot, d + 1)
                for n in range(4):
                    w = min(TC, NT - n * TC)
                    last = nc.vector.tensor_scalar(k.otile[d][0:1, n * TC:n * TC + w], pO[n][0:1, 0:w], -1.0, None, ALU.add)
                last.then_inc(s_hc, 1)

        @block.tensor
        def _(pe):
            pe.wait_ge(s_c, 4)
            nc.tensor.matmul(pH[0][:, 0:NO], zero[:], zero[:, 0:NO], start=True, stop=True)
            nc.tensor.matmul(pH[1][:, 0:NO], zero[:], zero[:, 0:NO], start=True, stop=True).then_inc(s_h, 1)
            with pe.Fori(0, NG // 2) as i:
                for par in range(2):
                    pe.wait_ge(s_oh, 2 * i + par + 1)
                    for d in range(2):
                        for t in range(SG):
                            last = nc.tensor.matmul(pH[d][:, 0:NO], oh_lo[:, par, d, :, t], oh_hi[:, par, d, :, t],
                                                    start=False, stop=True, skip_group_check=True)
                    last.then_inc(s_h, 1)
            for d in range(2):
                pe.wait_ge(s_hc, d + 1)
                nc.tensor.matmul(pO[0][:, 0:NO], k.below[:], hs[:, d, :], start=True, stop=True)
                nc.tensor.matmul(pO[1][:, 0:NO], k.ones[:], hs[:, d, :], start=True, stop=True).then_inc(s_o, 1)
                pe.wait_ge(s_oc, d + 1)
                for n in range(4):
                    w = min(TC, NT - n * TC)
                    last = nc.tensor.matmul(pO[n][0:1, 0:w], k.ones[0:NO, 0:1], ge[:, n * TC:n * TC + w], start=True, stop=True)
                last.then_inc(s_ot, 1)


def place_edges(nc, k, S, recs, raw, own, piece, ea, inval, ramp_hi, oh_lo, oh_hi, tri, sel, base):
    CT, SG, NO, NT, REC = S.CT, S.SG, S.NO, S.NT, S.REC
    NG, Q = CT // SG, S.SG // 4
    with ExitStack() as ctx:
        s = Scope(nc, ctx, "place")
        own_g = s.sb("own_g", [P, 2, 2, SG])
        piece_g = s.sb("piece_g", [P, 2, P], BF16)
        rec = s.sb("rec", [P, 2, 2, SG, REC])
        rows = s.sb("rows", [64, P], BF16)
        t_lo = s.sb("t_lo", [P, 8, P])
        cur = s.sb("cur", [P, 2, NO])
        junk = s.sb("junk", [P, 2, 4, P], BF16)
        prod = s.sb("prod", [P, 2, 8, NO])
        mark = s.sb("mark", [P, 2])
        below = s.sb("below", [P, 2, 2, SG])
        found = s.sb("found", [P, 2, 2, SG])
        slot = s.sb("slot", [P, 2, SG])
        slot_i = s.sb("slot_i", [P, 2, SG], I32)
        slot_l = s.sb("slot_l", [P, 2, SG], I32)
        addr = s.sb("addr", [P, 2, 2, SG], I32)
        pC = [s.pb(f"pC{d}") for d in range(2)]
        pT = s.pb("pT", [P, 8, P], BF16)
        pB = [s.pb(f"pB{d}", [P, 4, P]) for d in range(2)]
        pL = [s.pb(f"pL{n}") for n in range(2)]
        s_stage, s_oh, s_rowp, s_rows, s_tps, s_tlo, s_l, s_selr, s_addr, s_link, s_ohf = [
            s.sem(n) for n in ("stage", "oh", "rowp", "rows", "tps", "tlo", "l", "selr", "addr", "link", "ohf")]
        s_b, s_eq, s_cnt, s_cur = [[s.sem(f"{n}{d}") for d in range(2)] for n in ("b", "eq", "cnt", "cur")]
        s_turn = s.sem("turn")
        s_scat = [s.sem(f"scat{p}") for p in range(2)]
        block = ctx.enter_context(nc.Block())

        @block.scalar
        def _(act):
            act.wait_ge(s_addr, 1)
            for d in range(2):
                act.wait_ge(s_cnt[d], 1)
                nc.scalar.activation(cur[:, d, :], pC[d][:, 0:NO], ACT.Copy).then_inc(s_cur[d], 1)
            with act.Fori(0, NG // 2) as i:
                for par in range(2):
                    g = 2 * i + par
                    act.wait_ge(s_addr, g)
                    act.wait_ge(s_scat[par], i * (32 * SG))
                    act.wait_ge(s_rowp, g)
                    nc.scalar.activation(own_g[:, par], own[:, :, bass.ds(g * SG, SG)], ACT.Copy)
                    nc.scalar.activation(piece_g[:, par, 0:4 * SG].rearrange("p (d a t) -> p d a t", d=2, a=2), piece[:, :, :, bass.ds(g * SG, SG)], ACT.Copy).then_inc(s_stage, 1)
                    for d in range(2):
                        e = ea[:, bass.ds(g * SG, SG), :]
                        r = rec[:, par, d]
                        nc.scalar.activation(r[:, :, 0:1], e[:, :, 0:1], ACT.Copy)
                        nc.scalar.activation(r[:, :, 1:2], e[:, :, 1 + d:2 + d], ACT.Copy)
                        nc.scalar.activation(r[:, :, 2:3], e[:, :, 2 - d:3 - d], ACT.Copy)
                        nc.scalar.activation(r[:, :, 3:4], own[:, d, bass.ds(g * SG, SG)].unsqueeze(2), ACT.Copy)
                        last = nc.scalar.activation(r[:, :, 4:5].bitcast(I32), raw[:, 1 - d, bass.ds(g * SG, SG)].unsqueeze(2), ACT.Copy)
                    last.then_inc(s_stage, 1)
                    act.wait_ge(s_rowp, g + 1)
                    nc.scalar.activation(rows[:], pT[0:64, 0, :], ACT.Copy).then_inc(s_rows, 1)
                    for q in range(Q):
                        n = Q * g + q
                        act.wait_ge(s_tps, n + 1)
                        nc.scalar.activation(t_lo[:], pT[:], ACT.Copy).then_inc(s_tlo, 1)
                        for t in range(4):
                            for d in range(2):
                                act.wait_ge(s_cnt[d], 4 * n + t + 2)
                                nc.scalar.activation(cur[:, d, :], pC[d][:, 0:NO], ACT.Copy).then_inc(s_cur[d], 1)

        @block.tensor
        def _(pe):
            for d in range(2):
                nc.tensor.matmul(pC[d][:, 0:NO], k.ident[:], base[:, d, :], start=True, stop=True).then_inc(s_cnt[d], 1)
            with pe.Fori(0, NG // 2) as i:
                for par in range(2):
                    g = 2 * i + par
                    pe.wait_ge(s_stage, 2 * g + 1)
                    pe.wait_ge(s_tlo, Q * g)
                    nc.tensor.transpose(pT[:, 0, :], piece_g[:, par, :], k.ident_b[:]).then_inc(s_rowp, 1)
                    pe.wait_ge(s_rows, g + 1)
                    pe.wait_ge(s_oh, g + 1)
                    for q in range(Q):
                        n = Q * g + q
                        for d in range(2):
                            pe.wait_ge(s_eq[d], n)
                            for t in range(4):
                                last = nc.tensor.matmul(pB[d][:, t, :], sel[:, d * 16 + 4 * q + t, :], rows[:], start=True, stop=True)
                            last.then_inc(s_b[d], 1)
                        pe.wait_ge(s_tlo, n)
                        for t in range(4):
                            for d in range(2):
                                last = nc.tensor.transpose(pT[:, 2 * t + d, :], oh_lo[:, par, d, :, 4 * q + t], k.ident_b[:])
                        last.then_inc(s_tps, 1)
                        pe.wait_ge(s_tlo, n + 1)
                        pe.wait_ge(s_selr, n)
                        for t in range(4):
                            for d in range(2):
                                j = 2 * t + d
                                pe.wait_ge(s_cur[d], 4 * n + t + 1)
                                last = nc.tensor.matmul(pL[q % 2][:, j * NO:(j + 1) * NO], t_lo[:, j, :], cur[:, d, :], start=True, stop=True)
                                nc.tensor.matmul(pC[d][:, 0:NO], oh_lo[:, par, d, :, 4 * q + t], oh_hi[:, par, d, :, 4 * q + t],
                                                 start=False, stop=True, skip_group_check=True).then_inc(s_cnt[d], 1)
                        last.then_inc(s_l, 1)

        @block.vector
        def _(dve):
            nc.vector.memset(piece_g[:], 0.0).then_inc(s_addr, 1)
            nc.vector.memset(slot[:], 0.0).then_inc(s_selr, 1)
            PER = 2 * 5
            with dve.Fori(0, NG // 2) as i:
                link, n_link = chain(dve, s_link, i * PER)
                for par in range(2):
                    g = 2 * i + par
                    dve.wait_ge(s_l, Q * g)
                    one_hots(nc, S, k, oh_lo, oh_hi, piece, ramp_hi, par, g * SG).then_inc(s_oh, 1)
                    dve.wait_ge(s_stage, 2 * g + 1)
                    for q in range(Q):
                        n = Q * g + q
                        for d in range(2):
                            dve.wait_ge(s_b[d], n + 1)
                            for t in range(4):
                                c = 4 * q + t
                                last = nc.vector.scalar_tensor_tensor(
                                    out=junk[:, d, t, :], in0=pB[d][:, t, :], scalar=own_g[:, par, d, c:c + 1], in1=tri[:],
                                    op0=ALU.is_equal, op1=ALU.mult, accum_out=below[:, par, d, c:c + 1])
                            last.then_inc(s_eq[d], 1)
                        dve.wait_ge(s_l, n + 1)
                        nc.vector.tensor_tensor(prod[:, q % 2].rearrange("p (t d) o -> p t d o", d=2),
                                                pL[q % 2][:, 0:8 * NO].rearrange("p (t d o) -> p t d o", t=4, d=2),
                                                oh_hi[:, par, :, :, 4 * q:4 * q + 4].rearrange("p d o t -> p t d o"),
                                                ALU.mult).then_inc(s_selr, 1)
                        dve.wait_ge(s_selr, n + 2)
                        last = nc.vector.tensor_reduce(found[:, par, :, 4 * q:4 * q + 4].rearrange("p d t -> p t d"),
                                                       prod[:, q % 2].rearrange("p (t d) o -> p t d o", d=2), op=ALU.add, axis=AX)
                    link(last)
                    link(nc.vector.tensor_tensor(slot_i[:], below[:, par], found[:, par], ALU.add))
                    nc.vector.tensor_scalar(slot_l[:], slot_i[:], P - 1, None, ALU.bitwise_and)
                    link(nc.vector.tensor_scalar(slot_i[:], slot_i[:], 7, None, ALU.logical_shift_right))
                    link(nc.vector.scalar_tensor_tensor(out=slot[:], in0=slot_l[:], scalar=float(NT), in1=slot_i[:], op0=ALU.mult, op1=ALU.add))
                    dve.wait_ge(s_scat[par], i * (32 * SG))
                    link(nc.vector.tensor_tensor(addr[:, par], slot[:], bc(inval[:, bass.ds(g * SG, SG)], 1, 2), ALU.add))
                    nc.vector.tensor_copy(mark[:, par:par + 1], addr[:, par, 0, 0:1]).then_inc(s_addr, 1)
                assert n_link[0] == PER, n_link

        @block.gpsimd
        def _(pool):
            with pool.Fori(0, NG // 2) as i:
                for par in range(2):
                    pool.wait_ge(s_stage, 4 * i + 2 * par + 2)
                    pool.wait_ge(s_addr, 2 * i + par + 2)
                    pool.sem_inc(s_turn, 1)
                    for d in range(2):
                        for t in range(SG):
                            nc.gpsimd.indirect_dma_start(recs[d], bass.IndirectOffsetOnAxis(addr[:, par, d, t:t + 1], 0),
                                                         rec[:, par, d, t, :], None, bounds_check=P * NT - 1,
                                                         oob_is_err=False).then_inc(s_scat[par], 16)
            for par in range(2):
                pool.wait_ge(s_scat[par], (NG // 2) * 32 * SG)


def gather(nc, k, S, d, rec_d, table, spill, keys, att_d, w_time, b_time, other=None):
    NT, G, DK, PROJ, TD, H, REC, VW, ROW, NB = S.NT, S.G, S.DK, S.PROJ, S.TD, S.H, S.REC, S.VW, S.ROW, S.NB
    F3 = 3 * TD
    HF = G // 2 * F3
    QC = DK - TD
    with ExitStack() as ctx:
        s = Scope(nc, ctx, f"gather{d}")
        att = s.sb("att", [P, NB * 32, H])
        blk = s.sb("blk", [G * REC, G * F3])
        wb = s.sb("wb", [1, 2 * TD])
        bq = s.sb("bq", [1, F3])
        with ExitStack() as ctx2:
            prepare(nc, k, S, Scope(nc, ctx2, f"prep{d}"), d, rec_d, keys, w_time, b_time, blk, wb, bq, att)
        if other:
            weights(nc, k, S, 1 - d, other[1], att)
        with ExitStack() as ctx2:
            scores(nc, k, S, Scope(nc, ctx2, f"score{d}"), d, rec_d, table, spill, blk, att, other and other[0])
        with ExitStack() as ctx2:
            s3 = Scope(nc, ctx2, f"att{d}")
            attT = s3.sb("attT", [P, 2, 4, P])
            s_t, s_c, s_o = s3.sem("t"), s3.sem("c"), s3.sem("o")
            pA = [s3.pb(f"pA{n}", [P, 4, P]) for n in range(2)]
            block = ctx2.enter_context(nc.Block())
            loads = [list(range(b, min(b + 4, NB))) for b in range(0, NB, 4)]

            @block.tensor
            def _(pe):
                for n, bs in enumerate(loads):
                    if n >= 2:
                        pe.wait_ge(s_c, n - 1)
                    for j, b in enumerate(bs):
                        last = nc.tensor.transpose(pA[n % 2][:, j, :], att[:, b * 32:(b + 1) * 32, :].rearrange("p t h -> p (t h)"), k.ident[:])
                    last.then_inc(s_t, 1)

            @block.scalar
            def _(act):
                for n, bs in enumerate(loads):
                    act.wait_ge(s_t, n + 1)
                    if n >= 2:
                        act.wait_ge(s_o, 16 * (n - 1))
                    nc.scalar.activation(attT[:, n % 2, 0:len(bs), :], pA[n % 2][:, 0:len(bs), :], ACT.Copy).then_inc(s_c, 1)

            @block.sync
            def _(sp):
                v = att_d.rearrange("(b t) h e -> (t h) b e", t=32)
                for n, bs in enumerate(loads):
                    sp.wait_ge(s_c, n + 1)
                    if n:
                        sp.wait_ge(s_o, 16 * n)
                    sp.dma_start(v[:, bs[0]:bs[0] + len(bs), :], attT[:, n % 2, 0:len(bs), :]).then_inc(s_o, 16)
                sp.wait_ge(s_o, 16 * len(loads))


def prepare(nc, k, S, s, d, rec_d, keys, w_time, b_time, blk, wb, bq, att):
    NT, G, TD, REC, NB = S.NT, S.G, S.TD, S.REC, S.NB
    F3 = 3 * TD
    NK = NB * 32 // P + (NB * 32 % P > 0)
    rec = s.sb("rec", [P, NT, REC])
    lo_i = s.sb("lo_i", [P, NT], I32)
    key = s.sb("key", [P, NB * 32])
    keyT = s.sb("keyT", [P, -(-NB * 32 // P), P])
    pT = s.pb("pT", [P, 4, P])
    s_r, s_w, s_dve, s_blk, s_key, s_act, s_t, s_c, s_ko, s_ro = [
        s.sem(n) for n in ("r", "w", "dve", "blk", "key", "act", "t", "c", "ko", "ro")]
    block = s.ctx.enter_context(nc.Block())

    @block.sync
    def _(sp):
        sp.dma_start(rec[:], rec_d.rearrange("(p c) f -> p c f", p=P)).then_inc(s_r, 16)
        sp.dma_start(wb[:, 0:TD], w_time.unsqueeze(0)).then_inc(s_w, 16)
        sp.dma_start(wb[:, TD:2 * TD], b_time.unsqueeze(0)).then_inc(s_w, 16)
        sp.wait_ge(s_blk, 1)
        for t in range(G):
            for word, col in ((0, 1), (1, 0), (2, 2)):
                sp.dma_start(blk[t * REC + word:t * REC + word + 1, t * F3 + col * TD:t * F3 + (col + 1) * TD], wb[:, 0:TD]).then_inc(s_w, 16)
            sp.dma_start(blk[t * REC + 3:t * REC + 4, t * F3:(t + 1) * F3], bq[:]).then_inc(s_w, 16)
        for n in range(NK):
            w = min(P, NB * 32 - n * P)
            sp.wait_ge(s_c, n + 1)
            sp.dma_start(keys[n * P:n * P + w, :], keyT[0:w, n, :]).then_inc(s_ko, 16)
        sp.wait_ge(s_act, 1)
        sp.dma_start(rec_d.rearrange("(p c) f -> p c f", p=P), rec[:]).then_inc(s_ro, 16)
        sp.wait_ge(s_ro, 16)
        sp.wait_ge(s_ko, 16 * NK)
        sp.wait_ge(s_w, 32 + 64 * G)

    @block.vector
    def _(dve):
        link, _ = chain(dve, s_dve)
        link(nc.vector.memset(blk[:], 0.0))
        dve.wait_ge(s_w, 32)
        link(nc.vector.tensor_scalar(wb[:, 0:2 * TD], wb[:, 0:2 * TD], 1.0 / (2 * math.pi), None, ALU.mult))
        nc.vector.tensor_scalar(bq[:].rearrange("p (a b) -> p a b", a=3), bc(wb[:, TD:2 * TD], 1, 3), 0.25, None, ALU.add).then_inc(s_blk, 1)
        link(nc.vector.memset(key[:], -1.0))
        nc.vector.memset(att[:], 0.0)
        dve.wait_ge(s_r, 16)
        link(nc.vector.tensor_copy(key[:, 0:NT], rec[:, :, 3]))
        nc.vector.tensor_scalar(rec[:, :, 3], rec[:, :, 3], 0.0, 1.0, ALU.mult, ALU.add).then_inc(s_key, 1)
        link(nc.vector.tensor_copy(lo_i[:], key[:, 0:NT]))
        link(nc.vector.tensor_scalar(lo_i[:], lo_i[:], P - 1, None, ALU.bitwise_and))
        link(nc.vector.tensor_scalar(k.lo[d][:], key[:, 0:NT], 0.0, PAD_LO, ALU.is_lt, ALU.mult))
        link(nc.vector.tensor_tensor(k.lo[d][:], k.lo[d][:], lo_i[:], ALU.add))

    @block.tensor
    def _(pe):
        pe.wait_ge(s_key, 1)
        for n in range(NK):
            w = min(P, NB * 32 - n * P)
            if n:
                pe.wait_ge(s_c, n)
            nc.tensor.transpose(pT[0:w, 0, :], key[:, n * P:n * P + w], k.ident[:]).then_inc(s_t, 1)

    @block.scalar
    def _(act):
        act.wait_ge(s_r, 16)
        act.wait_ge(s_key, 1)
        nc.scalar.activation(rec[:, :, 0:3], rec[:, :, 0:3], ACT.Ln, bias=1.0).then_inc(s_act, 1)
        for n in range(NK):
            w = min(P, NB * 32 - n * P)
            act.wait_ge(s_t, n + 1)
            nc.scalar.activation(keyT[0:w, n, :], pT[0:w, 0, :], ACT.Copy).then_inc(s_c, 1)


def scores(nc, k, S, s, d, rec_d, table, spill, blk, att, other):
    NT, G, DK, PROJ, TD, H, REC, VW, ROW = S.NT, S.G, S.DK, S.PROJ, S.TD, S.H, S.REC, S.VW, S.ROW
    F3 = 3 * TD
    HG = G // 2
    QC = DK - TD
    NI = NT // (2 * G)
    row = [s.sb(f"row{n}", [P, G, ROW]) for n in range(2)]
    eq = [s.sb(f"eq{n}", [P, G, TD]) for n in range(2)]
    rec = [s.sb(f"rec{n}", [P, G, REC]) for n in range(2)]
    idx = [s.sb(f"idx{n}", [P, G], I32) for n in range(2)]
    logs = [s.sb(f"logs{n}", [P, P]) for n in range(2)]
    logT = [s.sb(f"logT{n}", [G * REC, P]) for n in range(2)]
    turns = s.sb("turns", [P, 2, HG, F3])
    frac = [s.sb(f"frac{n}", [P, G, F3]) for n in range(2)]
    oh = [s.sb(f"oh{n}", [P, P, G], BF16) for n in range(2)]
    ohT = [s.sb(f"ohT{n}", [P, G, P]) for n in range(2)]
    prod = s.sb("prod", [P, G, H, DK])
    pX = s.pb("pX")
    pU = [pX[:, 0:HG * F3].rearrange("p (t f) -> p t f", f=F3), s.pb("pU", [P, HG, F3])[:]]
    XT = HG * F3
    pO = s.pb("pO", [P, G, P], BF16)
    pQ = [s.pb(f"pQ{n}", [P, G, DK]) for n in range(2)]
    (s_lg, s_lt, s_ltc, s_oh, s_ot, s_otc, s_q, s_att, s_link) = [
        s.sem(n) for n in ("lg", "lt", "ltc", "oh", "ot", "otc", "q", "att", "link")]
    s_u, s_tu, s_fr = [[s.sem(f"{n}{h}") for h in range(2)] for n in ("u", "tu", "fr")]
    s_sin = s.sem("sin")
    s_rec, s_g, s_v = [[s.sem(f"{n}{h}") for h in range(2)] for n in ("rec", "g", "v")]
    s_idx = s.sem("idx")
    s_turn = s.sem("turn")
    s_prod = s.sem("prod")
    if other is not None:
        o_row = [s.sb(f"o_row{n}", [P, G, VW]) for n in range(2)]
        o_oh = [s.sb(f"o_oh{n}", [P, G, P]) for n in range(2)]
        o_off = s.sb("o_off", [P, G, P])
        o_neg = [s.sb(f"o_neg{n}", [P, G]) for n in range(2)]
        mark = s.sb("mark", [P, 1])
        pS = [s.pb(f"pS{n}", [P, 2, VW]) for n in range(2)]
        s_orow = [s.sem(f"orow{n}") for n in range(2)]
        s_w, s_p, s_add, s_ooh, s_neg, s_off = [s.sem(n) for n in ("w", "p", "add", "ooh", "neg", "off")]
    block = s.ctx.enter_context(nc.Block())
    rec_v = rec_d.rearrange("(p c) f -> p c f", p=P)

    def steps(eng, step):
        if NI > 1:
            with eng.Fori(0, NI - 1) as i:
                step(2 * i, 0, i, 2)
                step(2 * i + 1, 1, i, 2)
        step(2 * NI - 2, 0, NI - 1, 1)
        step(2 * NI - 1, 1, NI - 1, 0)

    @block.gpsimd
    def _(pool):
        with pool.Fori(0, NI) as i:
            for h in range(2):
                pool.wait_ge(s_idx, 2 * i + h + 1)
                pool.wait_ge(s_att, 2 * i + h + 1)
                pool.wait_ge(s_v[h], 32 * i)
                pool.sem_inc(s_turn, 1)
                for t in range(G):
                    nc.gpsimd.indirect_dma_start(row[h][:, t, 0:2 * PROJ], None, table,
                                                 bass.IndirectOffsetOnAxis(idx[h][:, t:t + 1], 0)).then_inc(s_g[h], 16)

    @block.sync
    def _(sp):
        def records(n, h):
            sp.dma_start(rec[h][:], rec_v[:, bass.ds(n * G, G), :]).then_inc(s_rec[h], 16)

        def other_rows(n, h):
            sp.wait_ge(s_p, n * HG)
            sp.dma_start(o_row[h][:], other[:, bass.ds(n * G, G), :]).then_inc(s_orow[h], 16)

        def step(n, h, turn, ahead):
            if ahead == 2:
                sp.wait_ge(s_idx, n + 1)
                sp.wait_ge(s_lg, n + 1)
                records(n + 2, h)
            sp.wait_ge(s_g[h], 16 * G * (turn + 1))
            sp.dma_start(spill[:, bass.ds(n * G, G), 0:PROJ], row[h][:, :, 0:PROJ]).then_inc(s_v[h], 16)
            sp.wait_ge(s_sin, n + 1)
            sp.dma_start(spill[:, bass.ds(n * G, G), PROJ:VW], row[h][:, :, 2 * PROJ:ROW]).then_inc(s_v[h], 16)
            if ahead == 2 and other is not None:
                other_rows(n + 2, h)

        for h in range(2):
            records(h, h)
        if other is not None:
            for h in range(2):
                other_rows(h, h)
        steps(sp, step)
        for h in range(2):
            sp.wait_ge(s_v[h], 32 * NI)

    @block.scalar
    def _(act):
        def records(n, h, turn):
            act.wait_ge(s_g[h], 16 * G * turn)
            act.wait_ge(s_rec[h], 16 * (turn + 1))
            nc.scalar.activation(idx[h][:], rec[h][:].bitcast(I32)[:, :, 4], ACT.Copy).then_inc(s_idx, 1)
            act.wait_ge(s_lt, n)
            nc.scalar.activation(logs[h][:, 0:G * REC], rec[h][:].rearrange("p t f -> p (t f)"), ACT.Copy).then_inc(s_lg, 1)

        def transposed(n, h):
            act.wait_ge(s_lt, n + 1)
            nc.scalar.activation(logT[h][:], pX[0:G * REC, XT:XT + P], ACT.Copy).then_inc(s_ltc, 1)
            act.wait_ge(s_ot, n + 1)
            act.wait_ge(s_q, n)
            nc.scalar.activation(ohT[h][:], pO[:], ACT.Copy).then_inc(s_otc, 1)

        def whole_turns(n):
            for u in range(2):
                act.wait_ge(s_u[u], n + 1)
                act.wait_ge(s_fr[u], n)
                nc.scalar.activation(turns[:, u], pU[u], ACT.Copy, bias=MAGIC).then_inc(s_tu[u], 1)

        def other_one_hots(n, h):
            nc.scalar.activation(o_neg[h][:], k.lo[1 - d][:, bass.ds(n * G, G)], ACT.Copy, scale=-1.0).then_inc(s_neg, 1)
            act.wait_ge(s_neg, n + 1)
            for t in range(G):
                last = nc.scalar.activation(o_off[:, t, :], k.ramp[:], ACT.Abs, bias=o_neg[h][:, t:t + 1])
            last.then_inc(s_off, 1)
            act.wait_ge(s_off, n + 1)
            act.wait_ge(s_p, n * HG)
            nc.scalar.activation(o_oh[h][:], o_off[:], ACT.Relu, bias=1.0, scale=-1.0).then_inc(s_ooh, 1)
            act.wait_ge(s_ooh, n + 1)

        def step(n, h, turn, ahead):
            act.wait_ge(s_fr[1], n + 1)
            act.wait_ge(s_v[h], 32 * turn)
            act.wait_ge(s_att, n + 1)
            nc.scalar.activation(row[h][:, :, 2 * PROJ:ROW], frac[h][:, :, 0:2 * TD], ACT.Sin, scale=-2 * math.pi)
            nc.scalar.activation(eq[h][:], frac[h][:, :, 2 * TD:F3], ACT.Sin, scale=-2 * math.pi).then_inc(s_sin, 1)
            if ahead:
                transposed(n + 1, 1 - h)
            if ahead == 2:
                records(n + 2, h, turn + 1)
            if ahead:
                if other is not None:
                    other_one_hots(n + 1, 1 - h)
                whole_turns(n + 1)

        act.wait_ge(s_att, 2)
        records(0, 0, 0)
        transposed(0, 0)
        records(1, 1, 0)
        if other is not None:
            other_one_hots(0, 0)
        whole_turns(0)
        steps(act, step)

    @block.tensor
    def _(pe):
        def transposes(n, h):
            pe.wait_ge(s_lg, n + 1)
            pe.wait_ge(s_fr[0], n)
            nc.tensor.transpose(pX[:, XT:XT + P], logs[h][:], k.ident[:]).then_inc(s_lt, 1)
            pe.wait_ge(s_oh, n + 1)
            pe.wait_ge(s_otc, n)
            for t in range(G):
                last = nc.tensor.transpose(pO[:, t, :], oh[h][:, :, t], k.ident_b[:])
            last.then_inc(s_ot, 1)

        def angles(n, h):
            pe.wait_ge(s_ltc, n + 1)
            for u in range(2):
                pe.wait_ge(s_fr[u], n)
                nc.tensor.matmul(pU[u].rearrange("p t f -> p (t f)"), logT[h][:], blk[:, u * HG * F3:(u + 1) * HG * F3],
                                 start=True, stop=True).then_inc(s_u[u], 1)

        def add_up(n, h, q):
            pe.wait_ge(s_add, n * HG + 2 * q + 2)
            for j in (2 * q, 2 * q + 1):
                for t in (2 * j, 2 * j + 1):
                    last = nc.tensor.matmul(pS[q][:, j % 2, :], o_oh[h][:, t, :], o_row[h][:, t, :],
                                            start=(t % 2 == 0), stop=(t % 2 == 1))
                last.then_inc(s_p, 1)

        def step(n, h, turn, ahead):
            _, tiles = nc.values_load_multi_w_load_instructions(
                k.otile[d][0:1, bass.ds(n * G, G)], engines=[nc.tensor.engine], min_val=0, max_val=S.NO - 1,
                skip_runtime_bounds_check_because="an owner's tile")
            pe.wait_ge(s_otc, n + 1)
            pe.wait_ge(s_att, n + 1)
            for t in range(G):
                last = nc.tensor.matmul(pQ[h][:, t, :], ohT[h][:, t, :], k.qs[:, bass.ds(tiles[t] * DK, DK)], start=True, stop=True)
            last.then_inc(s_q, 1)
            if ahead:
                transposes(n + 1, 1 - h)
            if other is not None:
                pe.wait_ge(s_ooh, n + 1)
                pe.wait_ge(s_w, n + 1)
                add_up(n, h, 0)
            if ahead:
                angles(n + 1, 1 - h)
            if other is not None:
                add_up(n, h, 1)

        if other is not None:
            nc.tensor.matmul(pS[0][:, 0, :], k.ident[:], k.acc[:, 0:VW], start=True, stop=True).then_inc(s_p, HG)
        transposes(0, 0)
        angles(0, 0)
        steps(pe, step)

    @block.vector
    def _(dve):
        nc.vector.memset(logs[0][:], 0.0).then_inc(s_att, 1)
        nc.vector.memset(logs[1][:], 0.0).then_inc(s_att, 1)
        if other is not None:
            nc.vector.memset(mark[:], 0.0).then_inc(s_add, HG)

        def own_one_hots(n, h):
            dve.wait_ge(s_ot, n)
            nc.vector.tensor_tensor(oh[h][:], bc(k.lo[d][:, bass.ds(n * G, G)], 1, P), k.ramp16[:, :, 0:G], ALU.is_equal).then_inc(s_oh, 1)

        def parts_of_turns(n, h):
            dve.wait_ge(s_sin, n)
            for u in range(2):
                dve.wait_ge(s_tu[u], n + 1)
                nc.vector.scalar_tensor_tensor(out=frac[h][:, u * HG:(u + 1) * HG, :], in0=turns[:, u], scalar=MAGIC, in1=pU[u],
                                               op0=ALU.subtract, op1=ALU.subtract).then_inc(s_fr[u], 1)

        def weigh(n, h, turn):
            dve.wait_ge(s_orow[h], 16 * (turn + 1))
            r = o_row[h][:, :, 0:H * DK].rearrange("p t (h f) -> p t h f", h=H)
            nc.vector.tensor_tensor(r, r, bc(att[:, bass.ds(n * G, G), :], 3, DK), ALU.mult).then_inc(s_w, 1)

        def add(n, q, tiles):
            dve.wait_ge(s_p, (n + 1) * HG + 2 * q + 2)
            for j in (2 * q, 2 * q + 1):
                dve.wait_ge(s_add, (n + 1) * HG + j)
                o = k.acc[:, bass.ds(tiles[2 * j] * VW, VW)]
                nc.vector.tensor_tensor(o, o, pS[q][:, j % 2, :], ALU.add).then_inc(s_add, 1)

        def step(n, h, turn, ahead):
            link, _ = chain(dve, s_link, n * 2)
            dve.wait_ge(s_q, n + 1)
            dve.wait_ge(s_sin, n + 1)
            link(nc.vector.tensor_tensor(pQ[h][:, :, QC:DK], pQ[h][:, :, QC:DK], eq[h][:], ALU.add))
            dve.wait_ge(s_g[h], 16 * G * (turn + 1))
            link(nc.vector.tensor_tensor(prod[:], row[h][:, :, PROJ:PROJ + H * DK].rearrange("p t (h f) -> p t h f", h=H),
                                         bc(pQ[h][:], 2, H), ALU.mult))
            dve.sem_inc(s_prod, 1)
            nc.vector.tensor_reduce(att[:, bass.ds(n * G, G), :], prod[:], op=ALU.add, axis=AX).then_inc(s_att, 1)
            if ahead == 2:
                own_one_hots(n + 2, h)
            if other is not None:
                if ahead:
                    weigh(n + 1, 1 - h, turn + h)
                _, tiles = nc.values_load_multi_w_load_instructions(
                    k.otile[1 - d][0:1, bass.ds(n * G, G)], engines=[nc.vector.engine], min_val=0, max_val=S.NO - 1,
                    skip_runtime_bounds_check_because="an owner's tile")
                add(n, 0, tiles)
            if ahead:
                parts_of_turns(n + 1, 1 - h)
            if other is not None:
                add(n, 1, tiles)

        own_one_hots(0, 0)
        own_one_hots(1, 1)
        if other is not None:
            weigh(0, 0, 0)
        parts_of_turns(0, 0)
        steps(dve, step)


def softmax(nc, k, S, d, att_d, keys, alpha_d):
    TP, SPn, H, NT2 = S.TP, S.SP, S.H, S.NT2
    C = TP * P
    SCALE = 1.0 / math.sqrt(S.DK)
    with ExitStack() as ctx:
        s = Scope(nc, ctx, f"soft{d}")
        a = s.sb("a", [SPn, H, C])
        m = s.sb("m", [SPn, H, C])
        v = s.sb("v", [SPn, H, C])
        key = s.sb("key", [SPn, C + 2])
        run = s.sb("run", [SPn, C + 1])
        low = s.sb("low", [SPn, C])
        stop = s.sb("stop", [SPn, C])
        ends = s.sb("ends", [SPn, 3 + 1, H])
        keep = s.sb("keep", [H, 3, P])
        carry = s.sb("carry", [H, P + 2])
        cin = s.sb("cin", [SPn, H])
        zero = s.sb("zero", [P, P])
        pE = s.pb("pE")
        pF = s.pb("pF")
        s_in, s_a, s_dve, s_sub, s_exp, s_c, s_t, s_e, s_f, s_o, s_k, s_x = [
            s.sem(n) for n in ("in", "a", "dve", "sub", "exp", "c", "t", "e", "f", "o", "k", "x")]
        block = ctx.enter_context(nc.Block())
        w = NT2 - SPn * TP
        NIN = 1 + 2 * (SPn > 1)

        @block.sync
        def _(sp):
            kv = keys.rearrange("t e -> (t e)")
            sp.wait_ge(s_k, 1)
            sp.dma_start(key[:, 1:C + 1], kv[0:SPn * C].rearrange("(p c) -> p c", p=SPn)).then_inc(s_in, 16)
            if SPn > 1:
                with nc.allow_non_contiguous_dma(reason="one word of each partition"):
                    sp.dma_start(key[1:SPn, 0:1], kv[0:SPn * C].rearrange("(p c) -> p c", p=SPn)[0:SPn - 1, C - 1:C]).then_inc(s_in, 16)
                    sp.dma_start(key[0:SPn - 1, C + 1:C + 2], kv[0:SPn * C].rearrange("(p c) -> p c", p=SPn)[1:SPn, 0:1]).then_inc(s_in, 16)
            for h in range(H):
                sp.dma_start(a[:, h, :].rearrange("p (t e) -> p t e", e=P),
                             att_d[0:SPn * TP, h, :].rearrange("(p t) e -> p t e", p=SPn)).then_inc(s_a, 16)
            for h in range(H):
                sp.wait_ge(s_o, h + 1)
                sp.dma_start(alpha_d[0:SPn * TP, h, :].rearrange("(p t) e -> p t e", p=SPn),
                             a[:, h, :].rearrange("p (t e) -> p t e", e=P)).then_inc(s_x, 16)
            nz = 0
            while nz * P < w * H:
                rest = alpha_d[SPn * TP:NT2, :, :].rearrange("t h e -> (t h) e")
                r = min(P, w * H - nz * P)
                sp.dma_start(rest[nz * P:nz * P + r, :], zero[0:r, :]).then_inc(s_x, 16)
                nz += 1
            sp.wait_ge(s_x, 16 * (H + nz))

        @block.tensor
        def _(pe):
            for f in range(3):
                pe.wait_ge(s_c, f + 1)
                nc.tensor.transpose(pE[0:H, f * P:f * P + SPn], ends[:, f, :], k.ident[0:SPn, 0:SPn]).then_inc(s_t, 1)
            for n in range(4):
                pe.wait_ge(s_c, 4 + n)
                nc.tensor.transpose(pE[0:H, 0:SPn], ends[:, 3, :], k.ident[0:SPn, 0:SPn]).then_inc(s_t, 1)
                pe.wait_ge(s_e, n + 1)
                src = carry[:, 0:SPn] if n % 2 == 0 else carry[:, 2:SPn + 2]
                nc.tensor.transpose(pF[0:SPn, 0:H], src, k.ident[0:H, 0:H]).then_inc(s_f, 1)

        @block.scalar
        def _(act):
            for h in range(H):
                act.wait_ge(s_sub, h + 1)
                nc.scalar.activation(a[:, h, :], a[:, h, :], ACT.Exp, scale=SCALE).then_inc(s_exp, 1)

        @block.vector
        def _(dve):
            link, _ = chain(dve, s_dve)
            link(nc.vector.memset(zero[:], 0.0))
            link(nc.vector.memset(key[:, 0:1], -2.0))
            nc.vector.memset(key[:, C + 1:C + 2], -2.0).then_inc(s_k, 1)
            dve.wait_ge(s_in, 16 * NIN)
            link(nc.vector.tensor_tensor(run[:], key[:, 1:C + 2], key[:, 0:C + 1], ALU.is_equal))
            link(nc.vector.tensor_scalar(low[:], run[:, 0:C], -LOW, LOW, ALU.mult, ALU.add))
            link(nc.vector.tensor_scalar(stop[:], run[:, 1:C + 1], -1.0, 1.0, ALU.mult, ALU.add))
            for f, src in enumerate((low[:, 0:C], run[:, 0:C], run[:, 1:C + 1])):
                link(nc.vector.tensor_reduce(cin[:, f:f + 1], src, op=ALU.min, axis=AX))
                nc.vector.tensor_copy(ends[:, f, :], cin[:, f:f + 1].broadcast_to([SPn, H])).then_inc(s_c, 1)
                dve.wait_ge(s_t, f + 1)
                link(nc.vector.tensor_copy(keep[:, f, 0:SPn], pE[0:H, f * P:f * P + SPn]))
            dve.wait_ge(s_a, 16 * H)

            def scans(n, back, data0, src, dst, form, first, op0, op1):
                def at(x):
                    return x[:, ::-1] if back else x
                for h in range(H):
                    last = nc.vector.tensor_tensor_scan(at(dst[:, h, :]), at(data0), at(src[:, h, :]), first, op0, op1)
                link(last)
                link(nc.vector.memset(carry[:], first))
                edge = 0 if back else C - 1
                nc.vector.tensor_copy(ends[:, 3, :], dst[:, :, edge]).then_inc(s_c, 1)
                dve.wait_ge(s_t, 4 + n)
                nc.vector.tensor_tensor_scan(at(carry[:, 1:SPn + 1]), at(keep[:, form, 0:SPn]), at(pE[0:H, 0:SPn]), first, op0, op1).then_inc(s_e, 1)
                dve.wait_ge(s_f, n + 1)
                link(nc.vector.tensor_copy(cin[:], pF[0:SPn, 0:H]))
                for h in range(H):
                    last = nc.vector.tensor_tensor_scan(at(dst[:, h, :]), at(data0), at(src[:, h, :]), cin[:, h:h + 1], op0, op1)
                link(last)

            def last_of_run(n):
                for h in range(H):
                    last = nc.vector.tensor_tensor(m[:, h, :], m[:, h, :], stop[:], ALU.mult)
                link(last)
                scans(n, True, run[:, 1:C + 1], m, v, 2, 0.0, ALU.mult, ALU.add)

            scans(0, False, low[:], a, m, 0, LOW, ALU.add, ALU.max)
            last_of_run(1)
            for h in range(H):
                nc.vector.tensor_tensor(a[:, h, :], a[:, h, :], v[:, h, :], ALU.subtract).then_inc(s_sub, 1)
            dve.wait_ge(s_exp, H)
            scans(2, False, run[:, 0:C], a, m, 1, 0.0, ALU.mult, ALU.add)
            last_of_run(3)
            for h in range(H):
                link(nc.vector.tensor_scalar(v[:, h, :], v[:, h, :], 1e-16, None, ALU.add))
                link(nc.vector.reciprocal(v[:, h, :], v[:, h, :]))
                nc.vector.tensor_tensor(a[:, h, :], a[:, h, :], v[:, h, :], ALU.mult).then_inc(s_o, 1)


def weights(nc, k, S, d, alpha_d, al):
    NB, H = S.NB, S.H
    with ExitStack() as ctx2:
        s2 = Scope(nc, ctx2, f"al{d}")
        alT = s2.sb("alT", [P, NB, P])
        s_i, s_t, s_c, s_z = s2.sem("i"), s2.sem("t"), s2.sem("c"), s2.sem("z")
        pA = [s2.pb(f"pA{n}", [P, 4, P]) for n in range(2)]
        block = ctx2.enter_context(nc.Block())
        loads = [list(range(b, min(b + 4, NB))) for b in range(0, NB, 4)]

        @block.sync
        def _(sp):
            sp.dma_start(alT[:], alpha_d.rearrange("(b t) h e -> (t h) b e", t=32)).then_inc(s_i, 16)

        @block.tensor
        def _(pe):
            pe.wait_ge(s_i, 16)
            for n, bs in enumerate(loads):
                if n >= 2:
                    pe.wait_ge(s_c, n - 1)
                for j, b in enumerate(bs):
                    last = nc.tensor.transpose(pA[n % 2][:, j, :], alT[:, b, :], k.ident[:])
                last.then_inc(s_t, 1)

        @block.scalar
        def _(act):
            for n, bs in enumerate(loads):
                act.wait_ge(s_t, n + 1)
                nc.scalar.activation(al[:, bs[0] * 32:(bs[-1] + 1) * 32, :].rearrange("p t h -> p (t h)"),
                                     pA[n % 2][:, 0:len(bs), :].rearrange("p b e -> p (b e)"), ACT.Copy).then_inc(s_c, 1)

        @block.vector
        def _(dve):
            if d == 0:
                nc.vector.memset(k.acc[:], 0.0)


def aggregate(nc, k, S, d, spill, alpha_d):
    NT, G, DK, H, VW, NT2 = S.NT, S.G, S.DK, S.H, S.VW, S.NT2
    NI = NT // (2 * G)
    with ExitStack() as ctx:
        al = Scope(nc, ctx, f"agg{d}").sb("al", [P, NT2, H])
        weights(nc, k, S, d, alpha_d, al)
        with ExitStack() as ctx2:
            s2 = Scope(nc, ctx2, f"sum{d}")
            row = [s2.sb(f"row{n}", [P, G, VW]) for n in range(2)]
            oh = [s2.sb(f"oh{n}", [P, G, P]) for n in range(2)]
            off = [s2.sb(f"off{n}", [P, G, P]) for n in range(2)]
            neg = [s2.sb(f"neg{n}", [P, G]) for n in range(2)]
            mark = s2.sb("mark", [P, 1])
            pS = [s2.pb(f"pS{n}") for n in range(8)]
            s_v = [s2.sem(f"v{n}") for n in range(2)]
            s_w, s_p, s_add, s_oh, s_neg, s_off = [s2.sem(n) for n in ("w", "p", "add", "oh", "neg", "off")]
            block = ctx2.enter_context(nc.Block())

            @block.sync
            def _(sp):
                with sp.Fori(0, NI) as i:
                    for h in range(2):
                        sp.wait_ge(s_p, (2 * i + h) * (G // 2))
                        sp.dma_start(row[h][:], spill[:, bass.ds((2 * i + h) * G, G), :]).then_inc(s_v[h], 16)

            @block.tensor
            def _(pe):
                nc.tensor.matmul(pS[0][:, 0:VW], k.ident[:], k.acc[:, 0:VW], start=True, stop=True).then_inc(s_p, G // 2)
                with pe.Fori(0, NI) as i:
                    for h in range(2):
                        n = 2 * i + h
                        pe.wait_ge(s_oh, n + 1)
                        pe.wait_ge(s_w, n + 1)
                        for t in range(G):
                            if t % 2 == 0:
                                pe.wait_ge(s_add, (n + 1) * (G // 2) + t // 2 - G // 2 + 1)
                            last = nc.tensor.matmul(pS[h * (G // 2) + t // 2][:, 0:VW], oh[h][:, t, :], row[h][:, t, :],
                                                    start=(t % 2 == 0), stop=(t % 2 == 1))
                            if t % 2:
                                last.then_inc(s_p, 1)

            @block.scalar
            def _(act):
                with act.Fori(0, NI) as i:
                    for h in range(2):
                        n = 2 * i + h
                        nc.scalar.activation(neg[h][:], k.lo[d][:, bass.ds(n * G, G)], ACT.Copy, scale=-1.0).then_inc(s_neg, 1)
                        act.wait_ge(s_neg, n + 1)
                        for t in range(G):
                            last = nc.scalar.activation(off[h][:, t, :], k.ramp[:], ACT.Abs, bias=neg[h][:, t:t + 1])
                        last.then_inc(s_off, 1)
                        act.wait_ge(s_off, n + 1)
                        act.wait_ge(s_p, n * (G // 2))
                        nc.scalar.activation(oh[h][:], off[h][:], ACT.Relu, bias=1.0, scale=-1.0).then_inc(s_oh, 1)

            @block.vector
            def _(dve):
                nc.vector.memset(mark[:], 0.0).then_inc(s_add, G)

                def weigh(n, h, turn):
                    dve.wait_ge(s_v[h], 16 * (turn + 1))
                    r = row[h][:, :, 0:H * DK].rearrange("p t (h f) -> p t h f", h=H)
                    nc.vector.tensor_tensor(r, r, bc(al[:, bass.ds(n * G, G), :], 3, DK), ALU.mult).then_inc(s_w, 1)

                def add(n, h):
                    _, tiles = nc.values_load_multi_w_load_instructions(
                        k.otile[d][0:1, bass.ds(n * G, G)], engines=[nc.vector.engine], min_val=0, max_val=S.NO - 1,
                        skip_runtime_bounds_check_because="an owner's tile")
                    for j in range(G // 2):
                        dve.wait_ge(s_p, (n + 1) * (G // 2) + j + 1)
                        dve.wait_ge(s_add, n * (G // 2) + G + j)
                        o = k.acc[:, bass.ds(tiles[2 * j] * VW, VW)]
                        nc.vector.tensor_tensor(o, o, pS[h * (G // 2) + j][:, 0:VW], ALU.add).then_inc(s_add, 1)

                weigh(0, 0, 0)
                if NI > 1:
                    with dve.Fori(0, NI - 1) as i:
                        weigh(2 * i + 1, 1, i)
                        add(2 * i, 0)
                        weigh(2 * i + 2, 0, i + 1)
                        add(2 * i + 1, 1)
                weigh(2 * NI - 1, 1, NI - 1)
                add(2 * NI - 2, 0)
                add(2 * NI - 1, 1)


def store_sums(nc, k, S, sums):
    OUT, NO, N = S.OUT, S.NO, S.N
    with ExitStack() as ctx:
        s = Scope(nc, ctx, "sums")
        s_o = s.sem("o")
        block = ctx.enter_context(nc.Block())

        @block.sync
        def _(sp):
            if NO > 1:
                sp.dma_start(sums[0:(NO - 1) * P, :].rearrange("(o p) f -> p o f", p=P),
                             k.acc[:, 0:(NO - 1) * OUT].rearrange("p (o f) -> p o f", f=OUT)).then_inc(s_o, 16)
            sp.dma_start(sums[(NO - 1) * P:N, :], k.acc[0:S.LAST, (NO - 1) * OUT:NO * OUT]).then_inc(s_o, 16)
            sp.wait_ge(s_o, 32 if NO > 1 else 16)


def output(nc, k, S, x, sums, Wa, ba, gamma, beta, out):
    T, OUT, IN, B, NBT, N = S.T, S.OUT, S.IN, S.B, S.NBT, S.N
    OC = OUT // P
    with ExitStack() as ctx:
        s = Scope(nc, ctx, "out")
        W = s.sb("W", [P, OC, T, IN])
        W2 = s.sb("W2", [P, T, IN])
        bias = s.sb("bias", [1, T, 3 * IN])
        idx = [s.sb(f"idx{h}", [P, B], I32) for h in range(2)]
        xr = [s.sb(f"xr{h}", [P, B, IN]) for h in range(2)]
        ag = [s.sb(f"ag{h}", [P, B, OUT]) for h in range(2)]
        z = [s.sb(f"z{h}", [P, B, IN]) for h in range(2)]
        aT = s.sb("aT", [P, B, OUT])
        y = s.sb("y", [P, B, IN])
        sq = s.sb("sq", [P, 2, B, IN])
        st = s.sb("st", [P, 7, B])
        pT = [s.pb(f"pT{n}", [P, 2, OUT]) for n in range(2)]
        pP = [s.pb(f"pP{n}", [P, 2, IN]) for n in range(2)]
        pG = [s.pb(f"pG{n}", [P, 2, IN]) for n in range(B)]
        s_w, s_w2, s_wr, s_clr, s_idx, s_aT, s_aTc, s_p, s_y, s_gb, s_z, s_link, s_mean, s_sq, s_var, s_root, s_turn = [
            s.sem(n) for n in ("w", "w2", "wr", "clr", "idx", "aT", "aTc", "p", "y", "gb", "z", "link", "mean", "sq", "var", "root", "turn")]
        s_g = [s.sem(f"g{h}") for h in range(2)]
        s_sc = [s.sem(f"sc{h}") for h in range(2)]
        block = ctx.enter_context(nc.Block())

        @block.sync
        def _(sp):
            for c in range(OC):
                sp.dma_start(W[:, c], Wa[:, c * P:(c + 1) * P, :].rearrange("t p n -> p t n")).then_inc(s_w, 16)
            for j, b in enumerate((ba, gamma, beta)):
                sp.dma_start(bias[:, :, j * IN:(j + 1) * IN], b.unsqueeze(0)).then_inc(s_w, 16)
            for c in range(OC):
                if c:
                    sp.wait_ge(s_wr, c)
                sp.dma_start(W2[:], Wa[:, OUT + c * P:OUT + (c + 1) * P, :].rearrange("t p n -> p t n")).then_inc(s_w2, 16)
            for h in range(2):
                sp.wait_ge(s_sc[h], 16 * B * (NBT // 2))

        @block.gpsimd
        def _(pool):
            def gathers(n, h):
                pool.wait_ge(s_idx, n + 1)
                pool.sem_inc(s_turn, 1)
                for j in range(B):
                    for to, of in ((ag, sums), (xr, x)):
                        nc.gpsimd.indirect_dma_start(to[h][:, j, :], None, of, bass.IndirectOffsetOnAxis(idx[h][:, j:j + 1], 0),
                                                     bounds_check=N - 1, oob_is_err=False).then_inc(s_g[h], 16)

            def body(n, h, turn, more):
                if more:
                    gathers(n + 1, 1 - h)
                pool.wait_ge(s_z, n + 1)
                pool.sem_inc(s_turn, 1)
                for j in range(B):
                    nc.gpsimd.indirect_dma_start(out, bass.IndirectOffsetOnAxis(idx[h][:, j:j + 1], 0), z[h][:, j, :], None,
                                                 bounds_check=N - 1, oob_is_err=False).then_inc(s_sc[h], 16)
            for b in (*xr, *ag):
                last = nc.gpsimd.memset(b[:], 0.0)
            last.then_inc(s_clr, 1)
            pool.wait_ge(s_clr, 1)
            gathers(0, 0)
            in_turns(pool, NBT, body)

        @block.tensor
        def _(pe):
            pe.wait_ge(s_wr, OC)

            def body(n, h, turn, more):
                types = tile_types(nc, k, S, nc.tensor, n)
                pe.wait_ge(s_g[h], 32 * B * (turn + 1))
                pe.wait_ge(s_aTc, 2 * n)
                for j in range(B):
                    for c in range(OC):
                        last = nc.tensor.transpose(pT[j // 2][:, j % 2, c * P:(c + 1) * P], ag[h][:, j, c * P:(c + 1) * P], k.ident[:])
                    if j % 2:
                        last.then_inc(s_aT, 1)
                flat = bias[:].rearrange("p t n -> p (t n)")
                pe.wait_ge(s_y, n)
                for j in range(B):
                    if j % 2 == 0:
                        pe.wait_ge(s_aTc, 2 * n + j // 2 + 1)
                    for c in range(OC):
                        nc.tensor.matmul(pP[j // 2][:, j % 2, :], aT[:, j, c * P:(c + 1) * P],
                                         W[:].rearrange("p c t n -> p c (t n)")[:, c, bass.ds(types[j] * IN, IN)],
                                         start=(c == 0), stop=False)
                    nc.tensor.matmul(pP[j // 2][:, j % 2, :], k.ones[0:1, :], flat[:, bass.ds(types[j] * (3 * IN), IN)],
                                     start=False, stop=True).then_inc(s_p, 1)
                pe.wait_ge(s_gb, n)
                for j in range(B):
                    nc.tensor.matmul(pG[j][:].rearrange("p a n -> p (a n)"), k.ones[0:1, :],
                                     flat[:, bass.ds(types[j] * (3 * IN) + IN, 2 * IN)], start=True, stop=True).then_inc(s_p, 1)
            in_turns(pe, NBT, body)

        @block.scalar
        def _(act):
            def stage(n, h, turn):
                act.wait_ge(s_sc[h], 16 * B * turn)
                nc.scalar.activation(idx[h][:], k.nodes[:, bass.ds(n * B, B)], ACT.Copy).then_inc(s_idx, 1)

            def body(n, h, turn, more):
                if more:
                    stage(n + 1, 1 - h, turn + h)
                for j in range(2):
                    act.wait_ge(s_aT, 2 * n + j + 1)
                    act.wait_ge(s_p, n * 2 * B)
                    nc.scalar.activation(aT[:, 2 * j:2 * j + 2, :], pT[j][:], ACT.Copy).then_inc(s_aTc, 1)
                for r in range(2):
                    act.wait_ge(s_mean, 2 * n + r + 1)
                    for j in range(B):
                        last = nc.scalar.activation(sq[:, r, j, :], y[:, j, :], ACT.Square, bias=st[:, 1, j:j + 1],
                                                    accum_out=st[:, 2, j:j + 1])
                    last.then_inc(s_sq, 1)
                    act.wait_ge(s_var, 2 * n + r + 1)
                    nc.scalar.activation(st[:, 4, :], st[:, 3, :], ACT.Sqrt).then_inc(s_root, 1)
            stage(0, 0, 0)
            in_turns(act, NBT, body)

        @block.vector
        def _(dve):
            dve.wait_ge(s_w, 16 * (OC + 3))
            for c in range(OC):
                dve.wait_ge(s_w2, 16 * (c + 1))
                nc.vector.tensor_tensor(W[:, c], W[:, c], W2[:], ALU.add).then_inc(s_wr, 1)
            PER = 7

            def body(n, h, turn, more):
                link, n_link = chain(dve, s_link, n * PER)

                def normalise(to, r, sem):
                    link(nc.vector.tensor_reduce(st[:, 0, :], y[:], op=ALU.add, axis=AX))
                    nc.vector.tensor_scalar(st[:, 1, :], st[:, 0, :], -1.0 / IN, None, ALU.mult).then_inc(s_mean, 1)
                    dve.wait_ge(s_sq, 2 * n + r + 1)
                    nc.vector.tensor_scalar(st[:, 3, :], st[:, 2, :], 1.0 / IN, LN_EPS, ALU.mult, ALU.add).then_inc(s_var, 1)
                    dve.wait_ge(s_root, 2 * n + r + 1)
                    link(nc.vector.reciprocal(st[:, 5, :], st[:, 4, :]))
                    for j in range(B):
                        last = nc.vector.tensor_scalar(to[:, j, :], y[:, j, :], st[:, 1, j:j + 1], st[:, 5, j:j + 1], ALU.add, ALU.mult)
                    if sem is None:
                        link(last)
                    else:
                        last.then_inc(sem, 1)

                for j in range(2):
                    dve.wait_ge(s_p, n * 2 * B + 2 * j + 2)
                    last = nc.vector.tensor_tensor(y[:, 2 * j:2 * j + 2, :], xr[h][:, 2 * j:2 * j + 2, :], pP[j][:], ALU.add)
                last.then_inc(s_y, 1)
                dve.wait_ge(s_y, n + 1)
                normalise(y, 0, None)
                dve.wait_ge(s_p, (n + 1) * 2 * B)
                for j in range(B):
                    last = nc.vector.tensor_tensor(y[:, j, :], y[:, j, :], pG[j][:, 0, :], ALU.mult)
                link(last)
                for j in range(B):
                    last = nc.vector.tensor_tensor(y[:, j, :], y[:, j, :], pG[j][:, 1, :], ALU.add)
                last.then_inc(s_gb, 1)
                dve.wait_ge(s_gb, n + 1)
                link(nc.vector.tensor_tensor(y[:], y[:], xr[h][:], ALU.add))
                dve.wait_ge(s_sc[h], 16 * B * turn)
                normalise(z[h], 1, s_z)
                dve.wait_ge(s_z, n + 1)
                assert n_link[0] == PER, n_link
            in_turns(dve, NBT, body)


class Kept:
    pass


def gnn_resnorm(nc, x, src, dst, edge_attr_5, node_type_19, Wk, bk, Wq, bq, Wv, bv, Wa, ba, gamma, beta, w_time, b_time, out):
    Scope.held = []
    S = Sizes(x, dst, Wk, Wa, w_time)
    recs = [nc.dram_tensor(f"recs{d}", [P * S.NT, S.REC], F32, kind="Internal").ap() for d in range(2)]
    slots = nc.dram_tensor("slots", [P * S.NTT, 1], I32, kind="Internal").ap()
    qtable = nc.dram_tensor("qtable", [S.N, S.DK], F32, kind="Internal").ap()
    sums = nc.dram_tensor("sums", [S.N, S.OUT], F32, kind="Internal").ap()
    table = nc.dram_tensor("table", [S.N, 2 * S.PROJ], F32, kind="Internal").ap()
    spill = [nc.dram_tensor(f"spill{d}", [P, S.NT, S.VW], F32, kind="Internal").ap() for d in range(2)]
    keys = [nc.dram_tensor(f"keys{d}", [S.NT2, P], F32, kind="Internal").ap() for d in range(2)]
    att = [nc.dram_tensor(f"att{d}", [S.NT2, S.H, P], F32, kind="Internal").ap() for d in range(2)]
    alpha = [nc.dram_tensor(f"alpha{d}", [S.NT2, S.H, P], F32, kind="Internal").ap() for d in range(2)]
    with ExitStack() as ctx:
        s = Scope(nc, ctx, "kept")
        k = Kept()
        k.ident = s.sb("ident", [P, P])
        k.ident_b = s.sb("ident_b", [P, P], BF16)
        k.ramp_i = s.sb("ramp_i", [P, P], I32)
        k.ramp = s.sb("ramp", [P, P])
        k.ones = s.sb("ones", [P, P])
        k.below = s.sb("below", [P, P])
        k.nodes = s.sb("nodes", [P, S.NTT], I32)
        k.ttype = s.sb("ttype", [1, S.NTT], I32)
        k.ramp16 = s.sb("ramp16", [P, P, S.SG], BF16)
        k.qs = s.sb("qs", [P, S.NO * S.DK])
        k.otile = [s.sb(f"otile{d}", [1, S.NT], I32) for d in range(2)]
        k.lo = [s.sb(f"lo{d}", [P, S.NT], BF16) for d in range(2)]
        constants(nc, k, S)
        group_nodes(nc, k, S, node_type_19, slots)
        project(nc, k, S, x, Wk, bk, Wq, bq, Wv, bv, table, qtable)
        Scope.retire(nc)
        sort_edges(nc, k, S, src, dst, edge_attr_5, recs)
        Scope.retire(nc)
        gather(nc, k, S, 0, recs[0], table, spill[0], keys[0], att[0], w_time, b_time)
        softmax(nc, k, S, 0, att[0], keys[0], alpha[0])
        Scope.retire(nc)
        with ExitStack() as ctx2:
            k.acc = Scope(nc, ctx2, "kept").sb("acc", [P, S.NO * S.OUT])
            gather(nc, k, S, 1, recs[1], table, spill[1], keys[1], att[1], w_time, b_time, (spill[0], alpha[0]))
            softmax(nc, k, S, 1, att[1], keys[1], alpha[1])
            Scope.retire(nc)
            aggregate(nc, k, S, 1, spill[1], alpha[1])
            store_sums(nc, k, S, sums)
        Scope.retire(nc)
        output(nc, k, S, x, sums, Wa, ba, gamma, beta, out)
        Scope.retire(nc)


_INS = ["x", "src", "dst", "edge_attr_5", "node_type_19", "L0_gnn_Wk", "L0_gnn_bk", "L0_gnn_Wq", "L0_gnn_bq", "L0_gnn_Wv",
        "L0_gnn_bv", "L0_gnn_Wa", "L0_gnn_ba", "L0_gnn_gamma", "L0_gnn_beta", "L0_gnn_w_time", "L0_gnn_b_time"]


def kernel(**inputs):
    import concourse.bacc as bacc
    from concourse.bass_utils import run_bass_kernel_spmd

    nc = bacc.Bacc("TRN2", target_bir_lowering=False, num_devices=1)
    arrays, args = {}, []
    for name in _INS:
        a = np.ascontiguousarray(inputs[name])
        arrays[f"in_{name}"] = a
        args.append(nc.dram_tensor(f"in_{name}", a.shape, mybir.dt.from_np(a.dtype), kind="ExternalInput").ap())
    out = nc.dram_tensor("out_x", inputs["x"].shape, F32, kind="ExternalOutput").ap()
    gnn_resnorm(nc, *args, out)
    r = run_bass_kernel_spmd(nc, [arrays], core_ids=[0])
    return r.results[0]["out_x"]
```
